# Optimizing a Trainium2 kernel written in Bass

```python
import numpy as np
import jax
import jax.numpy as jnp

def _softmax(x, axis=-1):
    return jax.nn.softmax(x, axis=axis)

def _gelu(x):
    return jax.nn.gelu(x, approximate=True)

def _silu(x):
    return jax.nn.silu(x)

def _sigmoid(x):
    return jax.nn.sigmoid(x)

def _layernorm(x, axis=-1, eps=1e-05):
    m = jnp.mean(x, axis=axis, keepdims=True)
    v = jnp.var(x, axis=axis, keepdims=True)
    return (x - m) / jnp.sqrt(v + eps)

def _scatter_add(tgt, idx, src, axis=0):
    return tgt.at[idx].add(src)

def _segment_sum(src, seg, n):
    return jax.ops.segment_sum(src, seg, n)
kernel_name = 'mk_decoder_postln_d4_seqx_r8_1b4884'

def setup_inputs(seed: int=0):
    np.random.seed(seed)
    _w = jnp.asarray

    def _rec_inputs():
        import jax
        import jax.numpy as jnp
        _rk = jax.random.key(seed)
        x = -0.0003929 + 0.9999 * jax.random.normal(jax.random.fold_in(_rk, 1), (128, 64, 128), jnp.float32)
        _lenS = 64 - jax.random.randint(jax.random.fold_in(_rk, 7), (128,), 0, max(1, 64 // 4) + 1, jnp.int32)
        _lenS2 = 64 - jax.random.randint(jax.random.fold_in(_rk, 8), (128,), 0, max(1, 64 // 4) + 1, jnp.int32)
        _ctx_1024P = jax.random.normal(jax.random.fold_in(_rk, 11), (128, 16, 128), jnp.float32)
        _ctx_1024c = jax.random.dirichlet(jax.random.fold_in(_rk, 511), 0.3 * jnp.ones((16,), jnp.float32), (128, 64))
        _ctx_1024t = jnp.einsum('bsk,bkd->bsd', _ctx_1024c, _ctx_1024P)
        _ctx_1024t = _ctx_1024t * jax.lax.rsqrt(jnp.mean(jnp.square(_ctx_1024t)) + 1e-12) * 0.953939
        ctx_1024 = 2.81802e-05 + 1.00001 * (_ctx_1024t + 0.3 * jax.random.normal(jax.random.fold_in(_rk, 611), (128, 64, 128), jnp.float32))
        _validS = jnp.arange(64)[None, :] < _lenS[:, None]
        _validS2 = jnp.arange(64)[None, :] < _lenS2[:, None]
        _causal = jnp.tril(jnp.ones((64, 64), dtype=bool))
        mask_BxS2_ik0 = jnp.where(jnp.broadcast_to(_validS2[:, :], (128, 64)), 0, 1).astype(jnp.int32)
        mask_Bx1xSxS2_bk0 = jnp.logical_not(jnp.broadcast_to(_validS2[:, None, None, :], (128, 1, 64, 64)))
        return (x, ctx_1024, mask_BxS2_ik0, mask_Bx1xSxS2_bk0)
    x, ctx_1024, mask_BxS2_ik0, mask_Bx1xSxS2_bk0 = _rec_inputs()

    def _L0_attn_setup():
        import jax, jax.numpy as jnp
        import numpy as np
        B, S, D = (4, 256, 128)
        F = 4 * D
        E = 8
        K = 2
        key = jax.random.key(seed)
        ks = jax.random.split(key, 4)
        s = 0.02
        return {'h_t': jax.random.normal(ks[0], (B, S, D), jnp.float32), 'gate_w': jax.random.normal(ks[1], (D, E), jnp.float32) * s, 'gate_b': jnp.zeros((E,), jnp.float32), 'w1': jax.random.normal(ks[2], (E, D, F), jnp.float32) * s, 'b1': jnp.zeros((E, F), jnp.float32), 'w2': jax.random.normal(ks[3], (E, F, D), jnp.float32) * s, 'b2': jnp.zeros((E, D), jnp.float32)}
    _L0_attn_all = _L0_attn_setup()
    _L0_attn_in = {k: v for k, v in _L0_attn_all.items() if k in ('gate_w', 'gate_b', 'w1', 'b1', 'w2', 'b2')}
    del _L0_attn_all

    def _L0_xattn_setup():
        import jax, jax.numpy as jnp
        import numpy as np
        DIM = 128
        B, TQ, TK = (8, 256, 256)
        key = jax.random.key(seed)
        ks = jax.random.split(key, 8)
        s = 1.0 / np.sqrt(DIM)
        return {'texto': jax.random.normal(ks[0], (B, TQ, DIM), dtype=jnp.float32), 'imagen': jax.random.normal(ks[1], (B, TK, DIM), dtype=jnp.float32), 'Wq': jax.random.normal(ks[2], (DIM, DIM), dtype=jnp.float32) * s, 'bq': jnp.zeros((DIM,), dtype=jnp.float32), 'Wk': jax.random.normal(ks[3], (DIM, DIM), dtype=jnp.float32) * s, 'bk': jnp.zeros((DIM,), dtype=jnp.float32), 'Wv': jax.random.normal(ks[4], (DIM, DIM), dtype=jnp.float32) * s, 'bv': jnp.zeros((DIM,), dtype=jnp.float32)}
    _L0_xattn_all = _L0_xattn_setup()
    _L0_xattn_in = {k: v for k, v in _L0_xattn_all.items() if k in ('Wq', 'bq', 'Wk', 'bk', 'Wv', 'bv')}
    del _L0_xattn_all

    def _L0_ffn_setup():
        import jax, jax.numpy as jnp
        import numpy as np
        EMB = 128
        FF = 4 * EMB

        def _ternary(w):
            scale = jnp.maximum(jnp.mean(jnp.abs(w)), 1e-08)
            w_t = jnp.clip(jnp.round(w / scale), -1.0, 1.0)
            return w + jax.lax.stop_gradient(w_t - w)
        key = jax.random.key(seed)
        kx, k1, k2, kb1, kb2 = jax.random.split(key, 5)
        x = jax.random.normal(kx, (4, 256, EMB), dtype=jnp.float32)
        lim1 = 1.0 / np.sqrt(EMB)
        lim2 = 1.0 / np.sqrt(FF)
        W1 = jax.random.uniform(k1, (FF, EMB), jnp.float32, -lim1, lim1)
        b1 = jax.random.uniform(kb1, (FF,), jnp.float32, -lim1, lim1)
        W2 = jax.random.uniform(k2, (EMB, FF), jnp.float32, -lim2, lim2)
        b2 = jax.random.uniform(kb2, (EMB,), jnp.float32, -lim2, lim2)
        return {'x': x, 'W1': W1, 'b1': b1, 'W2': W2, 'b2': b2}
    _L0_ffn_all = _L0_ffn_setup()
    _L0_ffn_in = {k: v for k, v in _L0_ffn_all.items() if k in ('W1', 'b1', 'W2', 'b2')}
    del _L0_ffn_all

    def _L1_attn_setup():
        import jax, jax.numpy as jnp
        import numpy as np
        import math
        B, T, E = (1, 256, 128)
        H = 8
        D = E // H // 2
        LAMBDA_INIT = 0.8 - 0.6 * math.exp(-0.3 * 1)
        SCALE_BASE = 512.0
        THETA = 10000.0

        def _rope_tables(T, d):
            inv_freq = 1.0 / THETA ** (jnp.arange(0, d, 2, dtype=jnp.float32) / d)
            pos = jnp.arange(T, dtype=jnp.float32)
            freqs = pos[:, None] * inv_freq[None, :]
            freqs = jnp.repeat(freqs, 2, axis=-1)
            sv = (jnp.arange(0, d, 2, dtype=jnp.float32) + 0.4 * d) / (1.4 * d)
            power = (pos - T // 2) / SCALE_BASE
            scale = sv[None, :] ** power[:, None]
            scale = jnp.concatenate([scale, scale], axis=-1)
            return (freqs, scale)

        def _rotate_half(x):
            x1 = x[..., 0::2]
            x2 = x[..., 1::2]
            return jnp.stack([-x2, x1], axis=-1).reshape(x.shape)

        def _apply_rope(t, freqs, scale):
            f = freqs[None, :, None, :]
            s = scale[None, :, None, :]
            return t * jnp.cos(f) * s + _rotate_half(t) * jnp.sin(f) * s
        key = jax.random.key(seed)
        ks = jax.random.split(key, 9)
        w = 0.02
        return {'x': jax.random.normal(ks[0], (B, T, E), dtype=jnp.float32), 'Wq': jax.random.normal(ks[1], (E, E), dtype=jnp.float32) * w, 'Wk': jax.random.normal(ks[2], (E, E), dtype=jnp.float32) * w, 'Wv': jax.random.normal(ks[3], (E, E), dtype=jnp.float32) * w, 'Wo': jax.random.normal(ks[4], (E, E), dtype=jnp.float32) * w, 'lambda_q1': jax.random.normal(ks[5], (D,), dtype=jnp.float32) * 0.1, 'lambda_k1': jax.random.normal(ks[6], (D,), dtype=jnp.float32) * 0.1, 'lambda_q2': jax.random.normal(ks[7], (D,), dtype=jnp.float32) * 0.1, 'lambda_k2': jax.random.normal(ks[8], (D,), dtype=jnp.float32) * 0.1}
    _L1_attn_all = _L1_attn_setup()
    _L1_attn_in = {k: v for k, v in _L1_attn_all.items() if k in ('Wq', 'Wk', 'Wv', 'Wo', 'lambda_q1', 'lambda_k1', 'lambda_q2', 'lambda_k2')}
    del _L1_attn_all

    def _L1_xattn_setup():
        import jax, jax.numpy as jnp
        import numpy as np
        E_PHI = 128
        E_F = 128
        HID = 128
        N_HEADS = 16
        HEAD_DIM = HID // N_HEADS
        key = jax.random.key(seed)
        ks = jax.random.split(key, 9)
        B, S = (2, 256)
        s = 0.02
        return {'q': jax.random.normal(ks[0], (B, S, E_PHI), jnp.float32), 'k': jax.random.normal(ks[1], (B, S, E_PHI), jnp.float32), 'v': jax.random.normal(ks[2], (B, S, E_F), jnp.float32), 'W_q': jax.random.normal(ks[3], (E_PHI, HID), jnp.float32) * s, 'W_k': jax.random.normal(ks[4], (E_PHI, HID), jnp.float32) * s, 'W_v': jax.random.normal(ks[5], (E_F, HID), jnp.float32) * s, 'b_v': jax.random.normal(ks[6], (HID,), jnp.float32) * s, 'W_o': jax.random.normal(ks[7], (HID, E_F), jnp.float32) * s, 'b_o': jax.random.normal(ks[8], (E_F,), jnp.float32) * s}
    _L1_xattn_all = _L1_xattn_setup()
    _L1_xattn_in = {k: v for k, v in _L1_xattn_all.items() if k in ('W_q', 'W_k', 'W_v', 'b_v', 'W_o', 'b_o')}
    del _L1_xattn_all

    def _L1_ffn_setup():
        import jax, jax.numpy as jnp
        import numpy as np
        B, K, D = (128, 32, 128)
        E = 32
        H = int(D * 0.25)

        def _rsqrt_uniform(key, shape, d):
            bound = d ** (-0.5)
            return jax.random.uniform(key, shape, jnp.float32, -bound, bound)
        key = jax.random.key(seed)
        ks = jax.random.split(key, 7)
        return {'x': jax.random.normal(ks[0], (B, K, D), jnp.float32), 'router_w': _rsqrt_uniform(ks[1], (E, D), D), 'router_b': _rsqrt_uniform(ks[2], (E,), D), 'weights1': _rsqrt_uniform(ks[3], (E, D, H), H), 'bias1': _rsqrt_uniform(ks[4], (E, H), H), 'weights2': _rsqrt_uniform(ks[5], (E, H, D), D), 'bias2': _rsqrt_uniform(ks[6], (E, D), D)}
    _L1_ffn_all = _L1_ffn_setup()
    _L1_ffn_in = {k: v for k, v in _L1_ffn_all.items() if k in ('router_w', 'router_b', 'weights1', 'bias1', 'weights2', 'bias2')}
    del _L1_ffn_all

    def _L2_attn_setup():
        import jax, jax.numpy as jnp
        import numpy as np
        EMBED = 128
        HEADS = 16
        GQA_GROUPS = 2
        KV_HEADS = HEADS // GQA_GROUPS
        HEAD_DIM = EMBED // HEADS
        ALIBI_ALPHA = 1.0
        START_I = 0
        N, S = (2, 256)

        def _alibi_bias(q_len, k_len):
            i = jnp.arange(1, HEADS + 1, dtype=jnp.float32)
            slopes = jnp.exp2(-ALIBI_ALPHA * (i + START_I)).reshape(1, HEADS, 1, 1)
            t_q = jnp.arange(q_len, dtype=jnp.float32)
            t_k = jnp.arange(k_len, dtype=jnp.float32)
            dist = jnp.abs(t_q[:, None] - t_k[None, :])
            return -dist[None, None] * slopes
        key = jax.random.key(seed)
        ks = jax.random.split(key, 6)
        x = jax.random.normal(ks[0], (N, S, EMBED), dtype=jnp.float32)
        sc = 1.0 / np.sqrt(EMBED)
        Wq = jax.random.normal(ks[1], (HEADS * HEAD_DIM, EMBED), dtype=jnp.float32) * sc
        Wk = jax.random.normal(ks[2], (KV_HEADS * HEAD_DIM, EMBED), dtype=jnp.float32) * sc
        Wv = jax.random.normal(ks[3], (KV_HEADS * HEAD_DIM, EMBED), dtype=jnp.float32) * sc
        Wo = jax.random.normal(ks[4], (EMBED, HEADS * HEAD_DIM), dtype=jnp.float32) * sc
        bo = jax.random.normal(ks[5], (EMBED,), dtype=jnp.float32) * 0.01
        return {'x': x, 'Wq': Wq, 'Wk': Wk, 'Wv': Wv, 'Wo': Wo, 'bo': bo}
    _L2_attn_all = _L2_attn_setup()
    _L2_attn_in = {k: v for k, v in _L2_attn_all.items() if k in ('Wq', 'Wk', 'Wv', 'Wo', 'bo')}
    del _L2_attn_all

    def _L2_xattn_setup():
        import jax, jax.numpy as jnp
        import numpy as np
        B, LQ, LK, D = (4, 256, 256, 128)
        H = 16
        HD = D // H

        def _split_heads(x):
            b, l, _ = x.shape
            return x.reshape(b, l, H, HD).transpose(0, 2, 1, 3)
        key = jax.random.key(seed)
        ks = jax.random.split(key, 10)
        s = 0.02
        return {'hidden_states': jax.random.normal(ks[0], (B, LQ, D), jnp.float32), 'context': jax.random.normal(ks[1], (B, LK, D), jnp.float32), 'attention_mask': jax.random.randint(ks[2], (B, LK), 0, 2, jnp.int32), 'q_w': jax.random.normal(ks[3], (D, D), jnp.float32) * s, 'q_b': jnp.zeros((D,), jnp.float32), 'k_w': jax.random.normal(ks[4], (D, D), jnp.float32) * s, 'k_b': jnp.zeros((D,), jnp.float32), 'v_w': jax.random.normal(ks[5], (D, D), jnp.float32) * s, 'v_b': jnp.zeros((D,), jnp.float32)}
    _L2_xattn_all = _L2_xattn_setup()
    _L2_xattn_in = {k: v for k, v in _L2_xattn_all.items() if k in ('q_w', 'q_b', 'k_w', 'k_b', 'v_w', 'v_b')}
    del _L2_xattn_all

    def _L2_ffn_setup():
        import jax, jax.numpy as jnp
        import numpy as np
        from jax import lax
        B, L, D = (4, 256, 128)
        E, TOPK = (8, 2)
        K, DIL = (3, 1)
        HID = D // 4
        EPS = 1e-06

        def _rmsnorm(h, w):
            rms = jnp.sqrt(jnp.mean(h * h, axis=-1, keepdims=True) + EPS)
            return w * (h / rms)

        def _forward(x, dw_kernel, dw_bias, pw_w, pw_b, router_w, router_b, expert_w, expert_b, out_w, out_b, norm_w, ff_down_w, ff_down_b, ff_up_w, ff_up_b):
            pad = (K - 1) * DIL
            xc = jnp.transpose(x, (0, 2, 1))
            xc = lax.conv_general_dilated(xc, dw_kernel, window_strides=(1,), padding=((pad, 0),), rhs_dilation=(DIL,), dimension_numbers=('NCH', 'OIH', 'NCH'), feature_group_count=D) + dw_bias[None, :, None]
            xc = jax.nn.silu(jnp.einsum('bdl,ed->bel', xc, pw_w) + pw_b[None, :, None])
            x1 = x + jnp.transpose(xc, (0, 2, 1))
            logits = jnp.einsum('bsd,ed->bse', x1, router_w) + router_b
            top_v, top_i = lax.top_k(logits, TOPK)
            top_w = jax.nn.softmax(top_v, axis=-1)
            rw = jnp.sum(jax.nn.one_hot(top_i, E, dtype=x1.dtype) * top_w[..., None], axis=-2)
            ye = jax.nn.silu(jnp.einsum('bsd,eod->bseo', x1, expert_w) + expert_b)
            combined = jnp.einsum('bse,bseo->bso', rw, ye)
            moe_out = jnp.einsum('bsd,od->bso', combined, out_w) + out_b
            h = _rmsnorm(x1 + moe_out, norm_w)
            ff = jax.nn.gelu(jnp.einsum('bsd,hd->bsh', h, ff_down_w) + ff_down_b, approximate=False)
            ff = jnp.einsum('bsh,dh->bsd', ff, ff_up_w) + ff_up_b
            return h + ff
        key = jax.random.key(seed)
        ks = jax.random.split(key, 16)
        s = 0.02
        return {'x': jax.random.normal(ks[0], (B, L, D), dtype=jnp.float32), 'dw_kernel': jax.random.normal(ks[1], (D, 1, K), dtype=jnp.float32) * s, 'dw_bias': jnp.zeros((D,), dtype=jnp.float32), 'pw_w': jax.random.normal(ks[2], (D, D), dtype=jnp.float32) * s, 'pw_b': jnp.zeros((D,), dtype=jnp.float32), 'router_w': jax.random.normal(ks[3], (E, D), dtype=jnp.float32) * s, 'router_b': jnp.zeros((E,), dtype=jnp.float32), 'expert_w': jax.random.normal(ks[4], (E, D, D), dtype=jnp.float32) * s, 'expert_b': jnp.zeros((E, D), dtype=jnp.float32), 'out_w': jax.random.normal(ks[5], (D, D), dtype=jnp.float32) * s, 'out_b': jnp.zeros((D,), dtype=jnp.float32), 'norm_w': jnp.ones((D,), dtype=jnp.float32), 'ff_down_w': jax.random.normal(ks[6], (HID, D), dtype=jnp.float32) * s, 'ff_down_b': jnp.zeros((HID,), dtype=jnp.float32), 'ff_up_w': jax.random.normal(ks[7], (D, HID), dtype=jnp.float32) * s, 'ff_up_b': jnp.zeros((D,), dtype=jnp.float32)}
    _L2_ffn_all = _L2_ffn_setup()
    _L2_ffn_in = {k: v for k, v in _L2_ffn_all.items() if k in ('dw_kernel', 'dw_bias', 'pw_w', 'pw_b', 'router_w', 'router_b', 'expert_w', 'expert_b', 'out_w', 'out_b', 'norm_w', 'ff_down_w', 'ff_down_b', 'ff_up_w', 'ff_up_b')}
    del _L2_ffn_all

    def _L3_attn_setup():
        import jax, jax.numpy as jnp
        import numpy as np
        EPS = 1e-12

        def _rmsnorm(x, gamma):
            d = gamma.shape[0]
            norm = jnp.sqrt(jnp.sum(x * x, axis=-1, keepdims=True))
            xn = x / jnp.maximum(norm, EPS)
            return xn * jnp.sqrt(jnp.asarray(d, x.dtype)) * gamma
        key = jax.random.key(seed)
        k1, k2 = jax.random.split(key)
        B, N, D = (4, 512, 128)
        x = jax.random.normal(k1, (B, N, D), dtype=jnp.float32)
        W_qkva = jax.random.normal(k2, (3 * D, D), dtype=jnp.float32) * 0.02
        gamma = jnp.ones((D,), dtype=jnp.float32)
        return {'x': x, 'W_qkva': W_qkva, 'gamma': gamma}
    _L3_attn_all = _L3_attn_setup()
    _L3_attn_in = {k: v for k, v in _L3_attn_all.items() if k in ('W_qkva', 'gamma')}
    del _L3_attn_all

    def _L3_xattn_setup():
        import jax, jax.numpy as jnp
        import numpy as np
        D = 128
        H = 16
        B = 4
        S = 256
        NEG = -1000000000.0
        key = jax.random.key(seed)
        ks = jax.random.split(key, 12)
        s = 0.02
        inp = {'Q': jax.random.normal(ks[0], (B, S, D), jnp.float32), 'K': jax.random.normal(ks[1], (B, S, D), jnp.float32), 'V': jax.random.normal(ks[2], (B, S, D), jnp.float32), 'mask': jnp.broadcast_to(jnp.tril(jnp.ones((S, S), bool)), (B, 1, S, S)), 'Wq': jax.random.normal(ks[3], (D, D), jnp.float32) * s, 'bq': jnp.zeros((D,), jnp.float32), 'Wk': jax.random.normal(ks[4], (D, D), jnp.float32) * s, 'bk': jnp.zeros((D,), jnp.float32), 'Wv': jax.random.normal(ks[5], (D, D), jnp.float32) * s, 'bv': jnp.zeros((D,), jnp.float32), 'Wo': jax.random.normal(ks[6], (D, D), jnp.float32) * s, 'bo': jnp.zeros((D,), jnp.float32)}
        return inp
    _L3_xattn_all = _L3_xattn_setup()
    _L3_xattn_in = {k: v for k, v in _L3_xattn_all.items() if k in ('Wq', 'bq', 'Wk', 'bk', 'Wv', 'bv', 'Wo', 'bo')}
    del _L3_xattn_all

    def _L3_ffn_setup():
        import jax, jax.numpy as jnp
        import numpy as np
        CAPACITY_FACTOR = 1.25
        key = jax.random.key(seed)
        k1, k2, k3, k4 = jax.random.split(key, 4)
        B, T, D, F, E = (4, 512, 128, 512, 8)
        s = 0.02
        return {'x': jax.random.normal(k1, (B, T, D), dtype=jnp.float32), 'wg': jax.random.normal(k2, (D, E), dtype=jnp.float32) * s, 'W1': jax.random.normal(k3, (E, D, F), dtype=jnp.float32) * s, 'b1': jnp.zeros((E, F), dtype=jnp.float32), 'W2': jax.random.normal(k4, (E, F, D), dtype=jnp.float32) * s, 'b2': jnp.zeros((E, D), dtype=jnp.float32)}
    _L3_ffn_all = _L3_ffn_setup()
    _L3_ffn_in = {k: v for k, v in _L3_ffn_all.items() if k in ('wg', 'W1', 'b1', 'W2', 'b2')}
    del _L3_ffn_all
    return {'x': x, 'ctx_1024': ctx_1024, 'mask_BxS2_ik0': mask_BxS2_ik0, 'mask_Bx1xSxS2_bk0': mask_Bx1xSxS2_bk0, 'L0_attn_gate_w': _L0_attn_in['gate_w'], 'L0_attn_gate_b': _L0_attn_in['gate_b'], 'L0_attn_w1': _L0_attn_in['w1'], 'L0_attn_b1': _L0_attn_in['b1'], 'L0_attn_w2': _L0_attn_in['w2'], 'L0_attn_b2': _L0_attn_in['b2'], 'L0_xattn_Wq': _L0_xattn_in['Wq'], 'L0_xattn_bq': _L0_xattn_in['bq'], 'L0_xattn_Wk': _L0_xattn_in['Wk'], 'L0_xattn_bk': _L0_xattn_in['bk'], 'L0_xattn_Wv': _L0_xattn_in['Wv'], 'L0_xattn_bv': _L0_xattn_in['bv'], 'L0_ffn_W1': _L0_ffn_in['W1'], 'L0_ffn_b1': _L0_ffn_in['b1'], 'L0_ffn_W2': _L0_ffn_in['W2'], 'L0_ffn_b2': _L0_ffn_in['b2'], 'L1_attn_Wq': _L1_attn_in['Wq'], 'L1_attn_Wk': _L1_attn_in['Wk'], 'L1_attn_Wv': _L1_attn_in['Wv'], 'L1_attn_Wo': _L1_attn_in['Wo'], 'L1_attn_lambda_q1': _L1_attn_in['lambda_q1'], 'L1_attn_lambda_k1': _L1_attn_in['lambda_k1'], 'L1_attn_lambda_q2': _L1_attn_in['lambda_q2'], 'L1_attn_lambda_k2': _L1_attn_in['lambda_k2'], 'L1_xattn_W_q': _L1_xattn_in['W_q'], 'L1_xattn_W_k': _L1_xattn_in['W_k'], 'L1_xattn_W_v': _L1_xattn_in['W_v'], 'L1_xattn_b_v': _L1_xattn_in['b_v'], 'L1_xattn_W_o': _L1_xattn_in['W_o'], 'L1_xattn_b_o': _L1_xattn_in['b_o'], 'L1_ffn_router_w': _L1_ffn_in['router_w'], 'L1_ffn_router_b': _L1_ffn_in['router_b'], 'L1_ffn_weights1': _L1_ffn_in['weights1'], 'L1_ffn_bias1': _L1_ffn_in['bias1'], 'L1_ffn_weights2': _L1_ffn_in['weights2'], 'L1_ffn_bias2': _L1_ffn_in['bias2'], 'L2_attn_Wq': _L2_attn_in['Wq'], 'L2_attn_Wk': _L2_attn_in['Wk'], 'L2_attn_Wv': _L2_attn_in['Wv'], 'L2_attn_Wo': _L2_attn_in['Wo'], 'L2_attn_bo': _L2_attn_in['bo'], 'L2_xattn_q_w': _L2_xattn_in['q_w'], 'L2_xattn_q_b': _L2_xattn_in['q_b'], 'L2_xattn_k_w': _L2_xattn_in['k_w'], 'L2_xattn_k_b': _L2_xattn_in['k_b'], 'L2_xattn_v_w': _L2_xattn_in['v_w'], 'L2_xattn_v_b': _L2_xattn_in['v_b'], 'L2_ffn_dw_kernel': _L2_ffn_in['dw_kernel'], 'L2_ffn_dw_bias': _L2_ffn_in['dw_bias'], 'L2_ffn_pw_w': _L2_ffn_in['pw_w'], 'L2_ffn_pw_b': _L2_ffn_in['pw_b'], 'L2_ffn_router_w': _L2_ffn_in['router_w'], 'L2_ffn_router_b': _L2_ffn_in['router_b'], 'L2_ffn_expert_w': _L2_ffn_in['expert_w'], 'L2_ffn_expert_b': _L2_ffn_in['expert_b'], 'L2_ffn_out_w': _L2_ffn_in['out_w'], 'L2_ffn_out_b': _L2_ffn_in['out_b'], 'L2_ffn_norm_w': _L2_ffn_in['norm_w'], 'L2_ffn_ff_down_w': _L2_ffn_in['ff_down_w'], 'L2_ffn_ff_down_b': _L2_ffn_in['ff_down_b'], 'L2_ffn_ff_up_w': _L2_ffn_in['ff_up_w'], 'L2_ffn_ff_up_b': _L2_ffn_in['ff_up_b'], 'L3_attn_W_qkva': _L3_attn_in['W_qkva'], 'L3_attn_gamma': _L3_attn_in['gamma'], 'L3_xattn_Wq': _L3_xattn_in['Wq'], 'L3_xattn_bq': _L3_xattn_in['bq'], 'L3_xattn_Wk': _L3_xattn_in['Wk'], 'L3_xattn_bk': _L3_xattn_in['bk'], 'L3_xattn_Wv': _L3_xattn_in['Wv'], 'L3_xattn_bv': _L3_xattn_in['bv'], 'L3_xattn_Wo': _L3_xattn_in['Wo'], 'L3_xattn_bo': _L3_xattn_in['bo'], 'L3_ffn_wg': _L3_ffn_in['wg'], 'L3_ffn_W1': _L3_ffn_in['W1'], 'L3_ffn_b1': _L3_ffn_in['b1'], 'L3_ffn_W2': _L3_ffn_in['W2'], 'L3_ffn_b2': _L3_ffn_in['b2']}

def reference(x, ctx_1024, mask_BxS2_ik0, mask_Bx1xSxS2_bk0, L0_attn_gate_w, L0_attn_gate_b, L0_attn_w1, L0_attn_b1, L0_attn_w2, L0_attn_b2, L0_xattn_Wq, L0_xattn_bq, L0_xattn_Wk, L0_xattn_bk, L0_xattn_Wv, L0_xattn_bv, L0_ffn_W1, L0_ffn_b1, L0_ffn_W2, L0_ffn_b2, L1_attn_Wq, L1_attn_Wk, L1_attn_Wv, L1_attn_Wo, L1_attn_lambda_q1, L1_attn_lambda_k1, L1_attn_lambda_q2, L1_attn_lambda_k2, L1_xattn_W_q, L1_xattn_W_k, L1_xattn_W_v, L1_xattn_b_v, L1_xattn_W_o, L1_xattn_b_o, L1_ffn_router_w, L1_ffn_router_b, L1_ffn_weights1, L1_ffn_bias1, L1_ffn_weights2, L1_ffn_bias2, L2_attn_Wq, L2_attn_Wk, L2_attn_Wv, L2_attn_Wo, L2_attn_bo, L2_xattn_q_w, L2_xattn_q_b, L2_xattn_k_w, L2_xattn_k_b, L2_xattn_v_w, L2_xattn_v_b, L2_ffn_dw_kernel, L2_ffn_dw_bias, L2_ffn_pw_w, L2_ffn_pw_b, L2_ffn_router_w, L2_ffn_router_b, L2_ffn_expert_w, L2_ffn_expert_b, L2_ffn_out_w, L2_ffn_out_b, L2_ffn_norm_w, L2_ffn_ff_down_w, L2_ffn_ff_down_b, L2_ffn_ff_up_w, L2_ffn_ff_up_b, L3_attn_W_qkva, L3_attn_gamma, L3_xattn_Wq, L3_xattn_bq, L3_xattn_Wk, L3_xattn_bk, L3_xattn_Wv, L3_xattn_bv, L3_xattn_Wo, L3_xattn_bo, L3_ffn_wg, L3_ffn_W1, L3_ffn_b1, L3_ffn_W2, L3_ffn_b2):
    import jax
    import jax.numpy as jnp

    def _L0_attn_ref(h_t, gate_w, gate_b, w1, b1, w2, b2):
        import jax, jax.numpy as jnp
        import numpy as np
        B, S, D = (4, 256, 128)
        F = 4 * D
        E = 8
        K = 2
        Bb, Ss, Dd = h_t.shape
        x = h_t.reshape(Bb * Ss, Dd)
        logits = x @ gate_w + gate_b
        probs = jax.nn.softmax(logits, axis=1)
        topw, topi = jax.lax.top_k(probs, K)
        topw = topw / topw.sum(axis=-1, keepdims=True)
        topw = topw.astype(h_t.dtype)
        hid = jax.nn.gelu(jnp.einsum('nd,edf->enf', x, w1) + b1[:, None, :])
        out = jnp.einsum('enf,efd->end', hid, w2) + b2[:, None, :]
        sel = topi[None, :, :] == jnp.arange(E)[:, None, None]
        ew = jnp.where(sel, topw[None, :, :], 0.0).sum(axis=-1)
        tmask = jnp.any(sel, axis=-1).astype(h_t.dtype)
        final = (out * ew[..., None] * tmask[..., None]).sum(axis=0)
        return final.reshape(Bb, Ss, Dd)

    def _L0_xattn_ref(texto, imagen, Wq, bq, Wk, bk, Wv, bv):
        import jax, jax.numpy as jnp
        import numpy as np
        DIM = 128
        B, TQ, TK = (8, 256, 256)
        q = texto @ Wq + bq
        k = imagen @ Wk + bk
        v = imagen @ Wv + bv
        scale = 1.0 / jnp.sqrt(jnp.asarray(texto.shape[-1], dtype=q.dtype))
        scores = jnp.einsum('bqd,bkd->bqk', q, k) * scale
        attn = jax.nn.softmax(scores, axis=-1)
        return jnp.einsum('bqk,bkd->bqd', attn, v)

    def _L0_ffn_ref(x, W1, b1, W2, b2):
        import jax, jax.numpy as jnp
        import numpy as np
        EMB = 128
        FF = 4 * EMB

        def _ternary(w):
            scale = jnp.maximum(jnp.mean(jnp.abs(w)), 1e-08)
            w_t = jnp.clip(jnp.round(w / scale), -1.0, 1.0)
            return w + jax.lax.stop_gradient(w_t - w)
        h = jnp.einsum('bsd,fd->bsf', x, _ternary(W1)) + b1
        h = jax.nn.gelu(h, approximate=False)
        out = jnp.einsum('bsf,df->bsd', h, _ternary(W2)) + b2
        return out

    def _L1_attn_ref(x, Wq, Wk, Wv, Wo, lambda_q1, lambda_k1, lambda_q2, lambda_k2):
        import jax, jax.numpy as jnp
        import numpy as np
        import math
        B, T, E = (1, 256, 128)
        H = 8
        D = E // H // 2
        LAMBDA_INIT = 0.8 - 0.6 * math.exp(-0.3 * 1)
        SCALE_BASE = 512.0
        THETA = 10000.0

        def _rope_tables(T, d):
            inv_freq = 1.0 / THETA ** (jnp.arange(0, d, 2, dtype=jnp.float32) / d)
            pos = jnp.arange(T, dtype=jnp.float32)
            freqs = pos[:, None] * inv_freq[None, :]
            freqs = jnp.repeat(freqs, 2, axis=-1)
            sv = (jnp.arange(0, d, 2, dtype=jnp.float32) + 0.4 * d) / (1.4 * d)
            power = (pos - T // 2) / SCALE_BASE
            scale = sv[None, :] ** power[:, None]
            scale = jnp.concatenate([scale, scale], axis=-1)
            return (freqs, scale)

        def _rotate_half(x):
            x1 = x[..., 0::2]
            x2 = x[..., 1::2]
            return jnp.stack([-x2, x1], axis=-1).reshape(x.shape)

        def _apply_rope(t, freqs, scale):
            f = freqs[None, :, None, :]
            s = scale[None, :, None, :]
            return t * jnp.cos(f) * s + _rotate_half(t) * jnp.sin(f) * s
        b, t, e = x.shape
        scaling = D ** (-0.5)
        q = (x @ Wq.T).reshape(b, t, 2 * H, D)
        k = (x @ Wk.T).reshape(b, t, 2 * H, D)
        v = (x @ Wv.T).reshape(b, t, H, 2 * D)
        freqs, scale = _rope_tables(t, D)
        q = _apply_rope(q, freqs, scale)
        k = _apply_rope(k, freqs, 1.0 / scale)
        q = jnp.transpose(q, (0, 2, 1, 3)) * scaling
        k = jnp.transpose(k, (0, 2, 1, 3))
        v = jnp.transpose(v, (0, 2, 1, 3))
        scores = jnp.einsum('bhtd,bhsd->bhts', q, k)
        probs = jax.nn.softmax(scores.astype(jnp.float32), axis=-1).astype(scores.dtype)
        lam1 = jnp.exp(jnp.sum(lambda_q1 * lambda_k1))
        lam2 = jnp.exp(jnp.sum(lambda_q2 * lambda_k2))
        lam = lam1 - lam2 + LAMBDA_INIT
        probs = probs.reshape(b, H, 2, t, t)
        diff = probs[:, :, 0] - lam * probs[:, :, 1]
        attn = jnp.einsum('bhts,bhsd->bhtd', diff, v)
        attn = attn * jax.lax.rsqrt(jnp.mean(attn * attn, axis=-1, keepdims=True) + 1e-05)
        attn = attn * (1.0 - LAMBDA_INIT)
        attn = jnp.transpose(attn, (0, 2, 1, 3)).reshape(b, t, e)
        return attn @ Wo.T

    def _L1_xattn_ref(q, k, v, W_q, W_k, W_v, b_v, W_o, b_o):
        import jax, jax.numpy as jnp
        import numpy as np
        E_PHI = 128
        E_F = 128
        HID = 128
        N_HEADS = 16
        HEAD_DIM = HID // N_HEADS
        B, S, _ = q.shape
        qh = (q @ W_q).reshape(B, S, N_HEADS, HEAD_DIM)
        kh = (k @ W_k).reshape(B, S, N_HEADS, HEAD_DIM)
        vh = (v @ W_v + b_v).reshape(B, S, N_HEADS, HEAD_DIM)
        scale = 1.0 / jnp.sqrt(jnp.float32(HEAD_DIM))
        scores = jnp.einsum('bihd,bjhd->bhij', qh, kh) * scale
        i = jnp.arange(S)[:, None]
        j = jnp.arange(S)[None, :]
        keep = (j < i) | (i == 0) & (j == 0)
        scores = jnp.where(keep, scores, jnp.float32(-jnp.inf))
        probs = jax.nn.softmax(scores, axis=-1)
        attn = jnp.einsum('bhij,bjhd->bihd', probs, vh).reshape(B, S, HID)
        return attn @ W_o + b_o

    def _L1_ffn_ref(x, router_w, router_b, weights1, bias1, weights2, bias2):
        import jax, jax.numpy as jnp
        import numpy as np
        B, K, D = (128, 32, 128)
        E = 32
        H = int(D * 0.25)

        def _rsqrt_uniform(key, shape, d):
            bound = d ** (-0.5)
            return jax.random.uniform(key, shape, jnp.float32, -bound, bound)
        b, k, d = x.shape
        x_flat = x.reshape(-1, d)
        n = x_flat.shape[0]
        logits = x_flat @ router_w.T + router_b
        routed_idx = jnp.argmax(logits, axis=-1)

        def expert_mlp(w1, b1, w2, b2):
            h = jax.nn.relu(x_flat @ w1 + b1)
            return jax.nn.relu(h @ w2 + b2)
        y_all = jax.vmap(expert_mlp)(weights1, bias1, weights2, bias2)
        out_flat = y_all[routed_idx, jnp.arange(n)]
        return out_flat.reshape(b, k, d)

    def _L2_attn_ref(x, Wq, Wk, Wv, Wo, bo):
        import jax, jax.numpy as jnp
        import numpy as np
        EMBED = 128
        HEADS = 16
        GQA_GROUPS = 2
        KV_HEADS = HEADS // GQA_GROUPS
        HEAD_DIM = EMBED // HEADS
        ALIBI_ALPHA = 1.0
        START_I = 0
        N, S = (2, 256)

        def _alibi_bias(q_len, k_len):
            i = jnp.arange(1, HEADS + 1, dtype=jnp.float32)
            slopes = jnp.exp2(-ALIBI_ALPHA * (i + START_I)).reshape(1, HEADS, 1, 1)
            t_q = jnp.arange(q_len, dtype=jnp.float32)
            t_k = jnp.arange(k_len, dtype=jnp.float32)
            dist = jnp.abs(t_q[:, None] - t_k[None, :])
            return -dist[None, None] * slopes
        n, s, _ = x.shape
        q = (x @ Wq.T).reshape(n, s, HEADS, HEAD_DIM)
        k = (x @ Wk.T).reshape(n, s, KV_HEADS, HEAD_DIM)
        v = (x @ Wv.T).reshape(n, s, KV_HEADS, HEAD_DIM)
        k = jnp.repeat(k, GQA_GROUPS, axis=2)
        v = jnp.repeat(v, GQA_GROUPS, axis=2)
        energy = jnp.einsum('nqhd,nkhd->nhqk', q, k)
        energy = energy + _alibi_bias(s, s)
        attn = jax.nn.softmax(energy / jnp.sqrt(jnp.float32(HEAD_DIM)), axis=-1)
        out = jnp.einsum('nhqk,nkhd->nqhd', attn, v).reshape(n, s, HEADS * HEAD_DIM)
        return out @ Wo.T + bo

    def _L2_xattn_ref(hidden_states, context, attention_mask, q_w, q_b, k_w, k_b, v_w, v_b):
        import jax, jax.numpy as jnp
        import numpy as np
        B, LQ, LK, D = (4, 256, 256, 128)
        H = 16
        HD = D // H

        def _split_heads(x):
            b, l, _ = x.shape
            return x.reshape(b, l, H, HD).transpose(0, 2, 1, 3)
        q = _split_heads(hidden_states @ q_w.T + q_b)
        k = _split_heads(context @ k_w.T + k_b)
        v = _split_heads(context @ v_w.T + v_b)
        scores = jnp.einsum('bhqd,bhkd->bhqk', q, k) / jnp.sqrt(jnp.float32(HD))
        mask = (attention_mask > 0)[:, None, None, :]
        scores = jnp.where(mask, -jnp.inf, scores)
        probs = jax.nn.softmax(scores, axis=-1)
        ctx = jnp.einsum('bhqk,bhkd->bhqd', probs, v)
        ctx = ctx.transpose(0, 2, 1, 3).reshape(ctx.shape[0], ctx.shape[2], H * HD)
        return ctx

    def _L2_ffn_ref(x, dw_kernel, dw_bias, pw_w, pw_b, router_w, router_b, expert_w, expert_b, out_w, out_b, norm_w, ff_down_w, ff_down_b, ff_up_w, ff_up_b):
        import jax, jax.numpy as jnp
        import numpy as np
        from jax import lax
        B, L, D = (4, 256, 128)
        E, TOPK = (8, 2)
        K, DIL = (3, 1)
        HID = D // 4
        EPS = 1e-06

        def _rmsnorm(h, w):
            rms = jnp.sqrt(jnp.mean(h * h, axis=-1, keepdims=True) + EPS)
            return w * (h / rms)

        def _forward(x, dw_kernel, dw_bias, pw_w, pw_b, router_w, router_b, expert_w, expert_b, out_w, out_b, norm_w, ff_down_w, ff_down_b, ff_up_w, ff_up_b):
            pad = (K - 1) * DIL
            xc = jnp.transpose(x, (0, 2, 1))
            xc = lax.conv_general_dilated(xc, dw_kernel, window_strides=(1,), padding=((pad, 0),), rhs_dilation=(DIL,), dimension_numbers=('NCH', 'OIH', 'NCH'), feature_group_count=D) + dw_bias[None, :, None]
            xc = jax.nn.silu(jnp.einsum('bdl,ed->bel', xc, pw_w) + pw_b[None, :, None])
            x1 = x + jnp.transpose(xc, (0, 2, 1))
            logits = jnp.einsum('bsd,ed->bse', x1, router_w) + router_b
            top_v, top_i = lax.top_k(logits, TOPK)
            top_w = jax.nn.softmax(top_v, axis=-1)
            rw = jnp.sum(jax.nn.one_hot(top_i, E, dtype=x1.dtype) * top_w[..., None], axis=-2)
            ye = jax.nn.silu(jnp.einsum('bsd,eod->bseo', x1, expert_w) + expert_b)
            combined = jnp.einsum('bse,bseo->bso', rw, ye)
            moe_out = jnp.einsum('bsd,od->bso', combined, out_w) + out_b
            h = _rmsnorm(x1 + moe_out, norm_w)
            ff = jax.nn.gelu(jnp.einsum('bsd,hd->bsh', h, ff_down_w) + ff_down_b, approximate=False)
            ff = jnp.einsum('bsh,dh->bsd', ff, ff_up_w) + ff_up_b
            return h + ff
        return _forward(x, dw_kernel, dw_bias, pw_w, pw_b, router_w, router_b, expert_w, expert_b, out_w, out_b, norm_w, ff_down_w, ff_down_b, ff_up_w, ff_up_b)

    def _L3_attn_ref(x, W_qkva, gamma):
        import jax, jax.numpy as jnp
        import numpy as np
        EPS = 1e-12

        def _rmsnorm(x, gamma):
            d = gamma.shape[0]
            norm = jnp.sqrt(jnp.sum(x * x, axis=-1, keepdims=True))
            xn = x / jnp.maximum(norm, EPS)
            return xn * jnp.sqrt(jnp.asarray(d, x.dtype)) * gamma
        xn = _rmsnorm(x, gamma)
        qkva = jnp.einsum('bnd,ed->bne', xn, W_qkva)
        q, kv, a = jnp.split(qkva, 3, axis=-1)
        a = jax.nn.sigmoid(a)

        def op(c1, c2):
            a_i, kv_i = c1
            a_j, kv_j = c2
            return (a_j * a_i, kv_j + a_j * kv_i)
        _, kv_scan = jax.lax.associative_scan(op, (a, kv), axis=1)
        out = q * kv_scan
        return out

    def _L3_xattn_ref(Q, K, V, mask, Wq, bq, Wk, bk, Wv, bv, Wo, bo):
        import jax, jax.numpy as jnp
        import numpy as np
        D = 128
        H = 16
        B = 4
        S = 256
        NEG = -1000000000.0
        d = D // H

        def split(x):
            Bx, Sx, _ = x.shape
            return x.reshape(Bx, Sx, H, d).transpose(0, 2, 1, 3)
        q = split(Q @ Wq + bq)
        k = split(K @ Wk + bk)
        v = split(V @ Wv + bv)
        scores = jnp.einsum('bhsd,bhtd->bhst', q, k) / jnp.sqrt(jnp.float32(d))
        scores = jnp.where(mask, scores, NEG)
        attn = jax.nn.softmax(scores, axis=-1)
        out = jnp.einsum('bhst,bhtd->bhsd', attn, v)
        out = out.transpose(0, 2, 1, 3).reshape(Q.shape[0], Q.shape[1], D)
        return out @ Wo + bo

    def _L3_ffn_ref(x, wg, W1, b1, W2, b2):
        import jax, jax.numpy as jnp
        import numpy as np
        CAPACITY_FACTOR = 1.25
        B, T, D = x.shape
        E = wg.shape[1]
        N = B * T
        capacity = int(N / E * CAPACITY_FACTOR) + 1
        xf = x.reshape(N, D)
        logits = xf @ wg
        scores = jax.nn.softmax(logits, axis=-1)
        top1 = jnp.argmax(scores, axis=-1)
        combine_w = jnp.take_along_axis(scores, top1[:, None], axis=1)[:, 0]
        oh = jax.nn.one_hot(top1, E, dtype=jnp.int32)
        rank = jnp.take_along_axis(jnp.cumsum(oh, axis=0), top1[:, None], axis=1)[:, 0] - 1
        valid = rank < capacity
        trash = E * capacity
        slot = jnp.where(valid, top1 * capacity + rank, trash)
        buf = jnp.zeros((E * capacity + 1, D), dtype=x.dtype).at[slot].set(xf)
        eb = buf[:E * capacity].reshape(E, capacity, D)
        h = jax.nn.gelu(jnp.einsum('ecd,edf->ecf', eb, W1) + b1[:, None, :], approximate=False)
        y = jnp.einsum('ecf,efd->ecd', h, W2) + b2[:, None, :]
        yf = y.reshape(E * capacity, D)
        gathered = yf[jnp.minimum(slot, E * capacity - 1)]
        out_flat = jnp.where(valid[:, None], gathered, 0.0) * combine_w[:, None]
        return out_flat.reshape(B, T, D)
    x = _layernorm(x + _L0_attn_ref(x, L0_attn_gate_w, L0_attn_gate_b, L0_attn_w1, L0_attn_b1, L0_attn_w2, L0_attn_b2), axis=-1)
    x = _layernorm(x + _L0_xattn_ref(x, ctx_1024, L0_xattn_Wq, L0_xattn_bq, L0_xattn_Wk, L0_xattn_bk, L0_xattn_Wv, L0_xattn_bv), axis=-1)
    x = _layernorm(x + _L0_ffn_ref(x, L0_ffn_W1, L0_ffn_b1, L0_ffn_W2, L0_ffn_b2), axis=-1)
    x = _layernorm(x + _L1_attn_ref(x, L1_attn_Wq, L1_attn_Wk, L1_attn_Wv, L1_attn_Wo, L1_attn_lambda_q1, L1_attn_lambda_k1, L1_attn_lambda_q2, L1_attn_lambda_k2), axis=-1)
    x = _layernorm(x + _L1_xattn_ref(x, ctx_1024, ctx_1024, L1_xattn_W_q, L1_xattn_W_k, L1_xattn_W_v, L1_xattn_b_v, L1_xattn_W_o, L1_xattn_b_o), axis=-1)
    x = _layernorm(x + _L1_ffn_ref(x, L1_ffn_router_w, L1_ffn_router_b, L1_ffn_weights1, L1_ffn_bias1, L1_ffn_weights2, L1_ffn_bias2), axis=-1)
    x = _layernorm(x + _L2_attn_ref(x, L2_attn_Wq, L2_attn_Wk, L2_attn_Wv, L2_attn_Wo, L2_attn_bo), axis=-1)
    x = _layernorm(x + _L2_xattn_ref(x, ctx_1024, mask_BxS2_ik0, L2_xattn_q_w, L2_xattn_q_b, L2_xattn_k_w, L2_xattn_k_b, L2_xattn_v_w, L2_xattn_v_b), axis=-1)
    x = _layernorm(x + _L2_ffn_ref(x, L2_ffn_dw_kernel, L2_ffn_dw_bias, L2_ffn_pw_w, L2_ffn_pw_b, L2_ffn_router_w, L2_ffn_router_b, L2_ffn_expert_w, L2_ffn_expert_b, L2_ffn_out_w, L2_ffn_out_b, L2_ffn_norm_w, L2_ffn_ff_down_w, L2_ffn_ff_down_b, L2_ffn_ff_up_w, L2_ffn_ff_up_b), axis=-1)
    x = _layernorm(x + _L3_attn_ref(x, L3_attn_W_qkva, L3_attn_gamma), axis=-1)
    x = _layernorm(x + _L3_xattn_ref(x, ctx_1024, ctx_1024, mask_Bx1xSxS2_bk0, L3_xattn_Wq, L3_xattn_bq, L3_xattn_Wk, L3_xattn_bk, L3_xattn_Wv, L3_xattn_bv, L3_xattn_Wo, L3_xattn_bo), axis=-1)
    x = _layernorm(x + _L3_ffn_ref(x, L3_ffn_wg, L3_ffn_W1, L3_ffn_b1, L3_ffn_W2, L3_ffn_b2), axis=-1)
    return x

_drawn_inputs = setup_inputs


def setup_inputs(seed=0):
    import zlib

    import numpy as np

    out = dict(_drawn_inputs(seed))
    spreads = {'L0_attn_gate_b': (0.0, 0.1),
     'L0_attn_b1': (0.0, 0.296),
     'L0_attn_b2': (0.0, 0.1),
     'L0_xattn_bq': (0.0, 0.1),
     'L0_xattn_bk': (0.0, 0.8),
     'L0_xattn_bv': (0.0, 0.1),
     'L2_xattn_q_b': (0.0, 0.8),
     'L2_xattn_k_b': (0.0, 0.8),
     'L2_xattn_v_b': (0.0, 0.1),
     'L2_ffn_dw_bias': (0.0, 0.8),
     'L2_ffn_pw_b': (0.0, 0.339),
     'L2_ffn_router_b': (0.0, 0.8),
     'L2_ffn_expert_b': (0.0, 0.8),
     'L2_ffn_out_b': (0.0, 0.1),
     'L2_ffn_norm_w': (1.0, 0.2),
     'L2_ffn_ff_down_b': (0.0, 0.8),
     'L2_ffn_ff_up_b': (0.0, 0.1),
     'L3_attn_gamma': (1.0, 0.58),
     'L3_xattn_bq': (0.0, 0.8),
     'L3_xattn_bk': (0.0, 0.8),
     'L3_xattn_bv': (0.0, 0.393),
     'L3_xattn_bo': (0.0, 0.1),
     'L3_ffn_b1': (0.0, 0.8),
     'L3_ffn_b2': (0.0, 0.67)}
    factors = {'L0_ffn_b1': 4.322,
     'L0_ffn_b2': 8.0,
     'L1_attn_Wq': 8.0,
     'L1_attn_Wk': 8.0,
     'L1_attn_lambda_q1': 8.0,
     'L1_attn_lambda_k1': 8.0,
     'L1_attn_lambda_q2': 8.0,
     'L1_attn_lambda_k2': 8.0,
     'L1_xattn_W_q': 8.0,
     'L1_xattn_W_k': 8.0,
     'L1_xattn_b_v': 3.971,
     'L1_ffn_bias1': 4.617,
     'L2_attn_bo': 5.455,
     'L2_xattn_q_w': 8.0,
     'L2_xattn_k_w': 8.0,
     'L2_ffn_dw_kernel': 8.0,
     'L2_ffn_pw_w': 8.0,
     'L2_ffn_router_w': 6.377,
     'L2_ffn_expert_w': 6.093,
     'L2_ffn_out_w': 5.611,
     'L2_ffn_ff_down_w': 8.0,
     'L2_ffn_ff_up_w': 8.0,
     'L3_xattn_Wq': 8.0,
     'L3_xattn_Wk': 8.0,
     'L3_ffn_wg': 3.602,
     'L3_ffn_W1': 8.0,
     'L3_ffn_W2': 8.0}
    for name, (base, spread) in spreads.items():
        noise = np.random.default_rng([zlib.crc32(name.encode()), seed]).standard_normal(out[name].shape)
        drawn = base * np.exp(spread * noise) if base else spread * noise
        out[name] = jnp.asarray(drawn.astype(out[name].dtype))
    for name, factor in factors.items():
        out[name] = (out[name] * factor).astype(out[name].dtype)
    return out
```

```python
import math
from contextlib import ExitStack

import numpy as np

import concourse.bass as bass
from concourse import mybir

N_SUBLAYERS = tuple(range(1, 13))

ALU = mybir.AluOpType
ACT = mybir.ActivationFunctionType
F32 = mybir.dt.float32
BF16 = mybir.dt.bfloat16
I32 = mybir.dt.int32
U8 = mybir.dt.uint8
U32 = mybir.dt.uint32
AX_X = mybir.AxisListType.X

B, S, D = 128, 64, 128
TOKENS = B * S
TILE = 128
TILES = TOKENS // TILE
CHUNK = 512
CHUNKS = TOKENS // CHUNK
PER = CHUNK // TILE
HEADS = 16
HD = D // HEADS
FF = 512
FB = FF // 128
EXPERTS = 8
LN_EPS = 1e-5
BIG = 3.0e38
LAMBDA_INIT = 0.8 - 0.6 * math.exp(-0.3)
CAPACITY = int(TOKENS / EXPERTS * 1.25) + 1


class Step:

    def __init__(self, i, u, per):
        self.i, self.u, self.per = i, u, per

    def shift(self, k):
        q, u = divmod(self.u + k, self.per)
        return Step(self.i + q if q else self.i, u, self.per)

    @property
    def n(self):
        return self.i * self.per + self.u

    @property
    def exists(self):
        return not isinstance(self.i, int) or self.i >= 0

    def inside(self, count):
        return not isinstance(self.i, int) or 0 <= self.n < count


SCRATCH = {}


def hold(eng):
    reg = SCRATCH[eng.engine]
    if eng.engine == mybir.EngineType.SP:
        eng.reg_add(reg, reg, 1)
        eng.reg_alu(reg, reg, 1, ALU.min)
    else:
        eng.reg_alu(reg, reg, 1, ALU.bitwise_or)


def done(step, times=1, extra=0):
    return step.n * times + times + extra


def nth(step, per, m):
    return step.n * per + m


def landed(step, dmas=1):
    n = step.n // 2 if isinstance(step.i, int) else step.i * (step.per // 2) + step.u // 2
    return (n + 1) * (16 * dmas)


class StepCount:

    def __init__(self, step, per):
        self.step, self.per, self.k = step, per, 0

    def next(self):
        self.k += 1
        assert self.k <= self.per
        return nth(self.step, self.per, self.k)


def run_loop(eng, per, count, body, first=2, last=1):
    turns = count // per
    for i in range(first):
        body(i)
    with eng.Fori(first, turns - last) as i:
        body(i)
    for i in range(turns - last, turns):
        body(i)


class Net:

    def __init__(self, nc, ctx, dram):
        self.nc, self.dram = nc, dram

        def sb(name, shape, dt=F32):
            return ctx.enter_context(nc.sbuf_tensor(name, shape, dt))

        self.x_tok = sb("x_tok", [128, TILES, D])
        self.x_T = sb("x_T", [128, TOKENS])
        self.ident = sb("ident", [128, 128])
        self.ones = sb("ones", [128, 128])
        self.minus_half = sb("minus_half", [128, 8])
        self.headmask = sb("headmask", [128, 8])
        self.sublayer_sems = []

    def semaphore(self, name):
        self.sublayer_sems.append(self.nc.alloc_semaphore(name))
        return self.sublayer_sems[-1]

    def end_sublayer(self):
        self.nc.clear_and_free_semaphores(self.sublayer_sems)
        self.nc.all_engine_barrier()
        self.sublayer_sems = []


def tile_cols(step, width=TILE):
    return bass.ds(step.n * width, width)


class Tail:

    def __init__(self, net, sb, sem, final):
        self.net, self.final = net, final
        self.r = sb("resid_sum", [128, 2, D])
        self.stats = sb("ln_stats", [128, 2, 6])
        self.mv = sb("ln_moments", [128, 2, 2])
        self.ve = sb("ln_var_eps", [128, 2, 1])
        self.rstd = sb("ln_rstd", [128, 2, 1])
        self.xn = sb("ln_out", [128, 2, D])
        self.xT = sb("ln_out_T", [128, 2, TILE])
        self.summed = sem("resid_summed")
        self.stats_done = sem("ln_stats_done")
        self.moments = sem("ln_moments_done")
        self.ve_done = sem("ln_var_eps_done")
        self.rstd_done = sem("ln_rstd_done")
        self.normed = sem("ln_normed")
        self.xT_ready = sem("ln_out_transposed")
        self.xT_copied = sem("ln_out_T_copied")
        self.stored = [sem("ln_stored_even"), sem("ln_stored_odd")]
        self.stores = 1 if final else 2

    def sum_and_moments(self, dve, t, y, x):
        p = t.u % 2
        if t.shift(-2).exists:
            dve.wait_ge(self.normed, done(t.shift(-2)))
        dve.tensor_tensor(self.r[:, p, :], y, x, ALU.add).then_inc(self.summed, 1)
        dve.wait_ge(self.summed, done(t))
        dve.bn_stats(self.stats[:, p, :], self.r[:, p, :]).then_inc(self.stats_done, 1)
        dve.wait_ge(self.stats_done, done(t))
        hold(dve)
        dve.bn_aggr(self.mv[:, p, :], self.stats[:, p, :]).then_inc(self.moments, 1)

    def inverse_std(self, pool, t):
        p = t.u % 2
        pool.wait_ge(self.moments, done(t))
        hold(pool)
        pool.tensor_scalar(self.ve[:, p, :], self.mv[:, p, 1:2], LN_EPS, None, ALU.add).then_inc(self.ve_done, 1)
        pool.wait_ge(self.ve_done, done(t))
        hold(pool)
        if t.shift(-2).exists:
            pool.wait_ge(self.normed, done(t.shift(-2)))
            hold(pool)
        pool.tensor_tensor(self.rstd[:, p, :], self.ve[:, p, :], self.net.minus_half[:, 0:1], ALU.pow)\
            .then_inc(self.rstd_done, 1)

    def normalise(self, dve, t):
        p = t.u % 2
        dve.wait_ge(self.rstd_done, done(t))
        if t.shift(-2).exists:
            dve.wait_ge(self.stored[t.shift(-2).u % 2], landed(t.shift(-2), self.stores))
        if not self.final:
            if t.shift(-2).exists:
                dve.wait_ge(self.xT_ready, done(t.shift(-2)))
        dve.tensor_scalar(self.xn[:, p, :], self.r[:, p, :], self.mv[:, p, 0:1], self.rstd[:, p, 0:1],
                          ALU.subtract, ALU.mult).then_inc(self.normed, 1)

    def transpose(self, pe, t, bank):
        if self.final:
            return
        pe.wait_ge(self.normed, done(t))
        if t.shift(-1).exists:
            pe.wait_ge(self.xT_copied, done(t.shift(-1)))
        pe.transpose(bank, self.xn[:, t.u % 2, :], self.net.ident[:, :]).then_inc(self.xT_ready, 1)

    def copy_transposed(self, act, t, bank):
        if self.final:
            return
        act.wait_ge(self.xT_ready, done(t))
        if t.shift(-2).exists:
            act.wait_ge(self.stored[t.shift(-2).u % 2], landed(t.shift(-2), self.stores))
        act.activation(self.xT[:, t.u % 2, :], bank, ACT.Copy).then_inc(self.xT_copied, 1)

    def store(self, sp, t):
        p = t.u % 2
        sp.wait_ge(self.normed, done(t))
        hold(sp)
        if self.final:
            sp.dma_start(self.net.dram["out"][bass.ds(t.n * TILE, TILE), :], self.xn[:, p, :]).then_inc(self.stored[p], 16)
            return
        sp.dma_start(self.net.x_tok[:, bass.ds(t.n, 1), :], self.xn[:, p:p + 1, :]).then_inc(self.stored[p], 16)
        sp.wait_ge(self.xT_copied, done(t))
        hold(sp)
        sp.dma_start(self.net.x_T[:, tile_cols(t)], self.xT[:, p, :]).then_inc(self.stored[p], 16)

    def all_stored(self, sp):
        for p in range(2):
            sp.wait_ge(self.stored[p], 16 * self.stores * TILES // 2)


def attention(net, final, name, wq, wk, wv, dv=HD, bq=None, bk=None, bv=None, wo=None, bo=None,
              cross=False, scale=1.0, mask=None, rope=False, lambdas=None):
    nc, dram = net.nc, net.dram
    W2 = 2 * (dv + 1)
    with ExitStack() as ctx:
        def sb(what, shape, dt=F32):
            return ctx.enter_context(nc.sbuf_tensor(f"{name}_{what}", shape, dt))

        def sem(what):
            return net.semaphore(f"{name}_{what}")

        def bank(what):
            return ctx.enter_context(nc.psum_tensor(f"{name}_{what}", [128, 512], F32))

        wq_s, wk_s = sb("wq", [128, 128]), sb("wk", [128, 128])
        wv_s = sb("wv", [128, 2, 8 * dv])
        bq_s, bk_s, bv_s = sb("bq", [128, 1]), sb("bk", [128, 1]), sb("bv", [128, 1])
        wqs_s, wks_s = sb("wq_swapped", [128, 128]), sb("wk_swapped", [128, 128])
        wo_s = sb("wo", [128, 128])
        add_row = sb("add_row", [128, D])
        table = sb("rope_table", [128, 4, 2, S]) if rope else None
        bias_const = None
        if mask and mask[1] == "causal":
            bias_const = sb("mask_const", [128, S])
        if mask and mask[0] == "add":
            bias_const = sb("mask_const", [128, HEADS * S])
        loads = []
        loads.append((wq_s[:, :], wq))
        if isinstance(wk, list):
            loads += [(wk_s[:, :].rearrange("p (k r d) -> p k r d", k=8, r=2)[:, :, r, :], w) for r, w in enumerate(wk)]
        else:
            loads.append((wk_s[:, :], wk))
        loads += [(wv_s[:, r, :] if len(w.shape) == 2 else wv_s[:, r, :].rearrange("p (k d) -> p k d", k=8), w)
                  for r, w in enumerate(wv)]
        if bq is not None:
            loads += [(bq_s[:, :], bq), (bk_s[:, :], bk)]
        if wo is not None:
            loads.append((wo_s[:, :], wo))
            if bv is not None:
                loads.append((bv_s[:, :], bv.rearrange("(p o) -> p o", o=1)))
        row = bo if wo is not None else bv
        if row is not None:
            loads.append((add_row[:, :], row.rearrange("(o n) -> o n", o=1).to_broadcast([128, D])))
        if rope:
            for dst, src in ((wqs_s, wq), (wks_s, wk)):
                for r in range(2):
                    loads.append((dst[:, :].rearrange("p (n r) -> p n r", r=2)[:, :, r],
                                  src.rearrange("p (n r) -> p n r", r=2)[:, :, 1 - r]))
            for b in range(2):
                loads.append((table[:, :, b, :], dram["c_rope"].rearrange("p (k s) -> p k s", k=4)))
        if mask and mask[1] == "causal":
            loads.append((bias_const[:, :], dram["c_causal"]))
        if mask and mask[0] == "add":
            loads.append((bias_const[:, :], dram[mask[1]]))

        x_in = sb("x_in", [128, 2, D])
        xT_in = sb("xT_in", [128, 2, TILE])
        cT_in = sb("cT_in", [128, 2, TILE]) if cross else xT_in
        x_res = sb("x_res", [128, 2, D]) if row is not None else x_in
        qk = sb("qk", [128, 2, 2, TILE])
        qk_parts = sb("qk_parts", [128, 4, TILE]) if rope else None
        k_blocks = sb("k_blocks", [128, 2, 8, TILE])
        v_blocks = sb("v_blocks", [128, 2, 2, 8, W2])
        probs = sb("probs", [128, 2, HEADS, S])
        bounded = sb("bounded", [128, HEADS, S]) if mask else None
        maxima = sb("maxima", [128, HEADS])
        probs_T = sb("probs_T", [128, 8, TILE])
        recip = sb("recip", [128, HEADS])
        o_heads = sb("o_heads", [128, HEADS, dv])
        o_T = sb("o_T", [128, TILE])
        if lambdas is not None:
            o_diff, o_sq = sb("o_diff", [128, 8, dv]), sb("o_sq", [128, 8, dv])
            o_norm = sb("o_norm", [128, 8, dv])
            ms, ms_eps, rms_inv = sb("ms", [128, 8]), sb("ms_eps", [128, 8]), sb("rms_inv", [128, 8])
            lam_in, lam_prod = sb("lam_in", [128, 4, HD]), sb("lam_prod", [128, 2, HD])
            lam_sum, lam_exp, neg_lam = sb("lam_sum", [128, 2]), sb("lam_exp", [128, 2]), sb("neg_lam", [128, 2])
            for k, v in enumerate(lambdas):
                loads.append((lam_in[:, k, :], v.rearrange("(o n) -> o n", o=1).to_broadcast([128, HD])))
        mask_tile = None
        if mask and mask[1] in ("keys", "full"):
            mask_in = sb("mask_in", [128, 2, S], I32 if mask[1] == "keys" else U8)
            mask_one = sb("mask_one", [128, 2, S])
            mask_tile = sb("mask_tile", [128, 2, S])
        n_loads = 1 + cross + (2 if mask and mask[1] == "keys" else 0) + (1 if mask and mask[1] == "full" else 0)

        score_bank = [bank("scores0"), bank("scores1")]
        qk_bank = bank("qk_ps")
        v_bank = bank("v_ps")
        pT_bank = [bank("pT0"), bank("pT1")]
        o_bank = bank("o_ps")
        tail_bank = bank("tail_ps")
        oT_ps, y_ps, xT_ps = tail_bank[:, 0:128], tail_bank[:, 128:256], tail_bank[:, 256:384]

        tail = Tail(net, sb, sem, final)
        weights = sem("weights_loaded")
        consts = sem("consts_ready")
        loaded = [sem("operands_loaded_even"), sem("operands_loaded_odd")]
        x_loaded = [sem("residual_loaded_even"), sem("residual_loaded_odd")]
        projected, v_projected = sem("qk_projected"), sem("v_projected")
        qk_copied, v_copied = sem("qk_copied"), sem("v_copied")
        spread = sem("keys_spread")
        scored = [sem("scores0_ready"), sem("scores1_ready")]
        bounded_s = sem("scores_bounded")
        max_done = sem("max_done")
        shifted = [sem("scores0_shifted"), sem("scores1_shifted")]
        exped = [sem("probs0_ready"), sem("probs1_ready")]
        turned = [sem("probs0_transposed"), sem("probs1_transposed")]
        turned_copied = [sem("probs0_T_copied"), sem("probs1_T_copied")]
        mixed = sem("values_mixed")
        o_steps = sem("output_steps")
        O_STEPS = 1 if lambdas is None else 6
        o_ready = sem("output_ready")
        ms_ready, ms_eps_done, rms_done = sem("ms_ready"), sem("ms_eps_done"), sem("rms_done")
        oT_ready, oT_copied, y_ready = sem("oT_ready"), sem("oT_copied"), sem("y_ready")
        biased, mask_ready, mask_step = sem("residual_biased"), sem("mask_ready"), sem("mask_step")
        rope_mult = sem("rope_multiplied")
        lam_steps = sem("lambda_steps")

        PERB = 2
        SUM = 0 if wo is None else 2
        NORM = 2 if wo is None else 3
        end = Step(TILES // 2, 0, PERB)

        def tile_loop(eng, turn):
            def body(i):
                for u in range(PERB):
                    turn(Step(i, u, PERB))
            run_loop(eng, PERB, TILES, body, first=3, last=2)

        o_out = o_heads[:, :, :].rearrange("p h d -> p (h d)") if lambdas is None else \
            o_norm[:, :, :].rearrange("p h d -> p (h d)")
        with nc.Block() as block:
            @block.sync
            def _(sp):
                for dst, src in loads:
                    with nc.allow_non_contiguous_dma(reason="weights, once"):
                        sp.dma_start(dst, src).then_inc(weights, 16)

                def load_operands(t):
                    p = t.u % 2
                    before = t.shift(-2)
                    if before.exists:
                        sp.wait_ge(v_projected, done(before))
                        hold(sp)
                    if mask_tile is not None:
                        if before.exists:
                            sp.wait_ge(mask_ready, done(before))
                            hold(sp)
                    sp.dma_start(xT_in[:, p, :], net.x_T[:, tile_cols(t)]).then_inc(loaded[p], 16)
                    if cross:
                        sp.dma_start(cT_in[:, p, :], dram["ctx_T"][:, tile_cols(t)]).then_inc(loaded[p], 16)
                    if mask and mask[1] == "keys":
                        for b in range(2):
                            sp.dma_start(mask_in[64 * b:64 * b + 64, p, :],
                                         dram["mask_keys"][bass.ds(t.n * 2 + b, 1), :].to_broadcast([64, S]))\
                                .then_inc(loaded[p], 16)
                    if mask and mask[1] == "full":
                        sp.dma_start(mask_in[:, p, :], dram["mask_full"][bass.ds(t.n * TILE, TILE), :])\
                            .then_inc(loaded[p], 16)

                def load_residual(t):
                    p = t.u % 2
                    if t.shift(-2).exists:
                        sp.wait_ge(biased if row is not None else tail.summed, done(t.shift(-2)))
                        hold(sp)
                    sp.dma_start(x_in[:, p:p + 1, :], net.x_tok[:, bass.ds(t.n, 1), :]).then_inc(x_loaded[p], 16)

                def turn(t):
                    if t.shift(3).inside(TILES):
                        load_operands(t.shift(3))
                    if t.shift(2 - SUM).inside(TILES):
                        load_residual(t.shift(2 - SUM))
                    if t.shift(-NORM).inside(TILES):
                        tail.store(sp, t.shift(-NORM))

                for n in range(3):
                    load_operands(end.shift(n - TILES))
                    if n < 2 - SUM:
                        load_residual(end.shift(n - TILES))
                tile_loop(sp, turn)
                for k in range(NORM):
                    tail.store(sp, end.shift(k - NORM))
                tail.all_stored(sp)

            @block.tensor
            def _(pe):
                pe.wait_ge(weights, 16 * len(loads))

                def project(t):
                    p = t.u % 2
                    pe.wait_ge(loaded[p], landed(t, n_loads))
                    if t.shift(-1).exists:
                        pe.wait_ge(qk_copied if not rope else rope_mult, done(t.shift(-1)))
                    products = [(wq_s, xT_in), (wk_s, cT_in)] + ([(wqs_s, xT_in), (wks_s, xT_in)] if rope else [])
                    for k, (w, src) in enumerate(products):
                        last = pe.matmul(qk_bank[:, 128 * k:128 * k + 128], w[:, :], src[:, p, :],
                                         start=True, stop=True)
                    last.then_inc(projected, 1)

                def project_values(t):
                    p = t.u % 2
                    if t.shift(-1).exists:
                        pe.wait_ge(v_copied, done(t.shift(-1), 2))
                    for b in range(2):
                        for r in range(2):
                            last = pe.matmul(v_bank[64 * r:64 * r + 64, 128 * b:128 * b + 8 * dv],
                                             cT_in[:, p, 64 * b:64 * b + 64], wv_s[:, r, :], start=True, stop=True)
                    last.then_inc(v_projected, 1)

                def scores(t):
                    pe.wait_ge(spread, done(t))
                    pe.wait_ge(qk_copied, done(t))
                    for g in range(2):
                        if t.shift(-1).exists:
                            if mask is None:
                                pe.wait_ge(shifted[g], done(t.shift(-1)))
                            else:
                                pe.wait_ge(bounded_s, done(t.shift(-1), 2, g - 1))
                        hold(pe)
                        for b in range(2):
                            last = pe.matmul(score_bank[g][64 * b:64 * b + 64, :],
                                             qk[64 * g:64 * g + 64, t.u % 2, 0, 64 * b:64 * b + 64],
                                             k_blocks[64 * g:64 * g + 64, t.u % 2, :, 64 * b:64 * b + 64],
                                             start=True, stop=True)
                        last.then_inc(scored[g], 1)

                def transpose_probs(t):
                    for g in range(2):
                        pe.wait_ge(exped[g], done(t))
                        if t.shift(-1).exists:
                            pe.wait_ge(turned_copied[g], done(t.shift(-1)))
                        for k in range(4):
                            h = 8 * g + 2 * k
                            last = pe.transpose(pT_bank[g][:, 128 * k:128 * k + 128],
                                                probs[:, t.u % 2, h:h + 2, :].rearrange("p h j -> p (h j)"),
                                                net.ident[:, :])
                        last.then_inc(turned[g], 1)

                def mix_values(t):
                    for g in range(2):
                        pe.wait_ge(turned_copied[g], done(t))
                    pe.wait_ge(v_copied, done(t, 2))
                    if lambdas is None:
                        if t.shift(-1).exists:
                            pe.wait_ge(o_ready, done(t.shift(-1)))
                    else:
                        if t.shift(-1).exists:
                            pe.wait_ge(o_steps, done(t.shift(-1), O_STEPS))
                    for b in range(2):
                        for k in range(8):
                            last = pe.matmul(o_bank[64 * b:64 * b + 64, W2 * k:W2 * k + W2],
                                             probs_T[:, k, 64 * b:64 * b + 64], v_blocks[:, t.u % 2, b, k, :],
                                             start=True, stop=True)
                    last.then_inc(mixed, 1)

                def turn_output(t):
                    if wo is not None:
                        if t.shift(-2).inside(TILES):
                            pe.wait_ge(tail.summed, done(t.shift(-2)))
                        if t.shift(-1).inside(TILES):
                            if not final and t.shift(-NORM - 1).exists:
                                pe.wait_ge(tail.xT_copied, done(t.shift(-NORM - 1)))
                            pe.wait_ge(o_ready, done(t.shift(-1)))
                            pe.transpose(oT_ps, o_out, net.ident[:, :]).then_inc(oT_ready, 1)
                    if t.shift(-NORM).inside(TILES):
                        tail.transpose(pe, t.shift(-NORM), xT_ps)

                def output(t):
                    if wo is None or not t.shift(-1).inside(TILES):
                        return
                    if not final and t.shift(-NORM).exists:
                        pe.wait_ge(tail.xT_copied, done(t.shift(-NORM)))
                    pe.wait_ge(oT_copied, done(t.shift(-1)))
                    pe.matmul(y_ps, o_T[:, :], wo_s[:, :], start=True, stop=True).then_inc(y_ready, 1)

                def turn(t):
                    if t.shift(1).inside(TILES):
                        project_values(t.shift(1))
                    if t.shift(2).inside(TILES):
                        project(t.shift(2))
                    if t.shift(1).inside(TILES):
                        scores(t.shift(1))
                    transpose_probs(t)
                    turn_output(t)
                    mix_values(t)
                    output(t)

                project(end.shift(-TILES))
                project_values(end.shift(-TILES))
                project(end.shift(1 - TILES))
                scores(end.shift(-TILES))
                tile_loop(pe, turn)
                for k in range(NORM):
                    turn_output(end.shift(k))
                    output(end.shift(k))

            @block.scalar
            def _(act):
                act.wait_ge(weights, 16 * len(loads))
                act.wait_ge(consts, 1)
                if lambdas is not None:
                    act.wait_ge(lam_steps, 2)
                    act.activation(lam_exp[:, :], lam_sum[:, :], ACT.Exp).then_inc(lam_steps, 1)

                def copy_projected(t):
                    p = t.u % 2
                    if rope:
                        return
                    act.wait_ge(projected, done(t))
                    if t.shift(-2).exists:
                        act.wait_ge(scored[1], done(t.shift(-2)))
                    if bq is not None:
                        act.activation(qk[:, p, 0, :], qk_bank[:, 0:128], ACT.Identity, bias=bq_s[:, 0:1])
                        act.activation(qk[:, p, 1, :], qk_bank[:, 128:256], ACT.Identity, bias=bk_s[:, 0:1])\
                            .then_inc(qk_copied, 1)
                    else:
                        act.activation(qk[:, p, :, :].rearrange("p a t -> p (a t)"), qk_bank[:, 0:256], ACT.Copy)\
                            .then_inc(qk_copied, 1)

                def copy_values(t):
                    act.wait_ge(v_projected, done(t))
                    if t.shift(-2).exists:
                        act.wait_ge(mixed, done(t.shift(-2)))
                    for r in range(2):
                        got = v_bank[64 * r:64 * r + 64, 0:256].rearrange("p (b x) -> p b x", b=2)[:, :, 0:8 * dv]
                        act.activation(v_blocks[64 * r:64 * r + 64, t.u % 2, :, :, r * (dv + 1):r * (dv + 1) + dv],
                                       got.rearrange("p b (k d) -> p b k d", k=8), ACT.Copy).then_inc(v_copied, 1)

                def copy_turned(t):
                    for g in range(2):
                        act.wait_ge(turned[g], done(t))
                        if t.shift(-1).exists:
                            act.wait_ge(mixed, done(t.shift(-1)))
                        act.activation(probs_T[:, 4 * g:4 * g + 4, :].rearrange("p k t -> p (k t)"), pT_bank[g][:, :],
                                       ACT.Copy).then_inc(turned_copied[g], 1)

                def exponentials(t):
                    for g in range(2):
                        act.wait_ge(shifted[g], done(t))
                        e = probs[:, t.u % 2, 8 * g:8 * g + 8, :].rearrange("p h j -> p (h j)")
                        act.activation(e, e, ACT.Exp, scale=scale).then_inc(exped[g], 1)

                def copy_output(t):
                    if wo is not None and t.shift(-1).inside(TILES):
                        act.wait_ge(oT_ready, done(t.shift(-1)))
                        if not final and t.shift(-NORM).exists:
                            act.wait_ge(tail.xT_ready, done(t.shift(-NORM)))
                        if t.shift(-2).exists:
                            act.wait_ge(y_ready, done(t.shift(-2)))
                        if bv is not None:
                            act.activation(o_T[:, :], oT_ps, ACT.Identity, bias=bv_s[:, 0:1]).then_inc(oT_copied, 1)
                        else:
                            act.activation(o_T[:, :], oT_ps, ACT.Copy).then_inc(oT_copied, 1)
                    if t.shift(-NORM).inside(TILES):
                        tail.copy_transposed(act, t.shift(-NORM), xT_ps)

                def turn(t):
                    if t.shift(1).inside(TILES):
                        copy_values(t.shift(1))
                    if t.shift(2).inside(TILES):
                        copy_projected(t.shift(2))
                    copy_turned(t)
                    copy_output(t)
                    if t.shift(1).inside(TILES):
                        exponentials(t.shift(1))

                copy_projected(end.shift(-TILES))
                copy_values(end.shift(-TILES))
                copy_projected(end.shift(1 - TILES))
                exponentials(end.shift(-TILES))
                tile_loop(act, turn)
                for k in range(NORM):
                    copy_output(end.shift(k))

            @block.vector
            def _(dve):
                dve.wait_ge(weights, 16 * len(loads))
                if lambdas is not None:
                    dve.tensor_tensor(lam_prod[:, :, :], lam_in[:, 0::2, :], lam_in[:, 1::2, :], ALU.mult)\
                        .then_inc(lam_steps, 1)
                    dve.wait_ge(lam_steps, 1)
                    dve.tensor_reduce(lam_sum[:, :], lam_prod[:, :, :], AX_X, ALU.add).then_inc(lam_steps, 1)
                    dve.wait_ge(lam_steps, 3)
                    dve.tensor_tensor(neg_lam[:, 0:1], lam_exp[:, 1:2], lam_exp[:, 0:1], ALU.subtract)\
                        .then_inc(lam_steps, 1)
                    dve.wait_ge(lam_steps, 4)
                    dve.tensor_scalar(neg_lam[:, 1:2], neg_lam[:, 0:1], LAMBDA_INIT, None, ALU.subtract)\
                        .then_inc(lam_steps, 1)
                    dve.wait_ge(lam_steps, 5)

                def rope_products(t):
                    dve.wait_ge(projected, done(t))
                    if t.shift(-1).exists:
                        dve.wait_ge(qk_copied, done(t.shift(-1)))
                    dve.tensor_tensor(qk_parts[:, :, :].rearrange("p a t -> p (a t)"), qk_bank[:, :],
                                      table[:, :, :, :].rearrange("p a b s -> p (a b s)"), ALU.mult)\
                        .then_inc(rope_mult, 1)

                def shift_scores(t):
                    p = t.u % 2
                    if mask_tile is not None:
                        dve.wait_ge(mask_ready, done(t))
                    for g in range(2):
                        heads = slice(8 * g, 8 * g + 8)
                        dve.wait_ge(scored[g], done(t))
                        src = score_bank[g][:, :].rearrange("p (h j) -> p h j", h=8)
                        if mask is not None:
                            if mask[0] == "add":
                                m = bias_const[:, 512 * g:512 * g + 512].rearrange("p (h j) -> p h j", h=8)
                            else:
                                one = bias_const[:, :] if mask_tile is None else mask_tile[:, p, :]
                                m = one.rearrange("p (o j) -> p o j", o=1).to_broadcast([128, 8, S])
                            dve.tensor_tensor(bounded[:, heads, :], src, m, ALU.add if mask[0] == "add" else ALU.min)\
                                .then_inc(bounded_s, 1)
                            dve.wait_ge(bounded_s, done(t, 2, g - 1))
                            src = bounded[:, heads, :]
                        dve.tensor_reduce(maxima[:, heads], src, AX_X, ALU.max).then_inc(max_done, 1)
                        dve.wait_ge(max_done, done(t, 2, g - 1))
                        if t.shift(-2).exists:
                            dve.wait_ge(turned[g], done(t.shift(-2)))
                        dve.tensor_tensor(probs[:, p, heads, :], src,
                                          maxima[:, heads].rearrange("p (h o) -> p h o", o=1).to_broadcast([128, 8, S]),
                                          ALU.subtract).then_inc(shifted[g], 1)

                def heads_output(t):
                    dve.wait_ge(mixed, done(t))
                    o_ps = o_bank[:, 0:HEADS * (dv + 1)].rearrange("p (h d) -> p h d", h=HEADS)
                    steps = StepCount(t, O_STEPS)
                    dve.reciprocal(recip[:, :], o_ps[:, :, dv:dv + 1].rearrange("p h o -> p (h o)")).then_inc(o_steps, 1)
                    dve.wait_ge(o_steps, steps.next())
                    hold(dve)
                    per_head = recip[:, :].rearrange("p (h o) -> p h o", o=1)
                    if lambdas is None:
                        if t.shift(-1).exists:
                            dve.wait_ge(oT_ready if wo is not None else tail.summed, done(t.shift(-1)))
                        dve.tensor_tensor(o_heads[:, :, :], o_ps[:, :, 0:dv], per_head.to_broadcast([128, HEADS, dv]),
                                          ALU.mult).then_inc(o_ready, 1)
                        return
                    odd = recip[:, :].rearrange("p (k r) -> p k r", r=2)[:, :, 1]
                    dve.tensor_scalar(odd, odd, neg_lam[:, 1:2], None, ALU.mult).then_inc(o_steps, 1)
                    dve.wait_ge(o_steps, steps.next())
                    hold(dve)
                    dve.tensor_tensor(o_heads[:, :, :], o_ps[:, :, 0:dv], per_head.to_broadcast([128, HEADS, dv]),
                                      ALU.mult).then_inc(o_steps, 1)
                    dve.wait_ge(o_steps, steps.next())
                    hold(dve)
                    pairs = o_heads[:, :, :].rearrange("p (k r) d -> p k r d", r=2)
                    dve.tensor_tensor(o_diff[:, :, :], pairs[:, :, 0, :], pairs[:, :, 1, :], ALU.add).then_inc(o_steps, 1)
                    dve.wait_ge(o_steps, steps.next())
                    hold(dve)
                    dve.tensor_tensor(o_sq[:, :, :], o_diff[:, :, :], o_diff[:, :, :], ALU.mult).then_inc(o_steps, 1)
                    dve.wait_ge(o_steps, steps.next())
                    hold(dve)
                    if t.shift(-1).exists:
                        dve.wait_ge(ms_eps_done, done(t.shift(-1)))
                    dve.tensor_reduce(ms[:, :], o_sq[:, :, :], AX_X, ALU.add).then_inc(o_steps, 1)
                    dve.wait_ge(o_steps, steps.next())
                    hold(dve)
                    dve.wait_ge(rms_done, done(t))
                    if t.shift(-1).exists:
                        dve.wait_ge(oT_ready, done(t.shift(-1)))
                    dve.tensor_tensor(o_norm[:, :, :], o_diff[:, :, :],
                                      rms_inv[:, :].rearrange("p (k o) -> p k o", o=1).to_broadcast([128, 8, dv]),
                                      ALU.mult).then_inc(o_ready, 1)

                def residual(t):
                    p = t.u % 2
                    if wo is not None:
                        dve.wait_ge(y_ready, done(t))
                    if row is not None:
                        dve.wait_ge(biased, done(t))
                    else:
                        dve.wait_ge(x_loaded[t.u % 2], landed(t))
                    tail.sum_and_moments(dve, t, y_ps if wo is not None else o_out, x_res[:, p, :])

                def add_and_normalise(t):
                    if wo is not None and t.shift(-SUM).inside(TILES):
                        residual(t.shift(-SUM))
                    if t.shift(-NORM).inside(TILES):
                        tail.normalise(dve, t.shift(-NORM))

                def turn(t):
                    if rope and t.shift(2).inside(TILES):
                        rope_products(t.shift(2))
                    add_and_normalise(t)
                    if t.shift(1).inside(TILES):
                        shift_scores(t.shift(1))
                    heads_output(t)
                    if wo is None:
                        dve.wait_ge(o_ready, done(t))
                        residual(t)

                if rope:
                    rope_products(end.shift(-TILES))
                    rope_products(end.shift(1 - TILES))
                shift_scores(end.shift(-TILES))
                tile_loop(dve, turn)
                for k in range(NORM):
                    add_and_normalise(end.shift(k))

            @block.gpsimd
            def _(pool):
                pool.wait_ge(weights, 16 * len(loads))
                flat = v_blocks[:, :, :, :, :].rearrange("p a b k w -> p (a b k) w")
                pool.memset(flat, 0.0).then_inc(mask_step, 1)
                pool.wait_ge(mask_step, 1)
                pool.memset(flat[0:64, :, dv:dv + 1], 1.0).then_inc(mask_step, 1)
                pool.wait_ge(mask_step, 2)
                pool.memset(flat[64:128, :, 2 * dv + 1:2 * dv + 2], 1.0).then_inc(consts, 1)

                def add_rope(t):
                    pool.wait_ge(rope_mult, done(t))
                    hold(pool)
                    if t.shift(-2).exists:
                        pool.wait_ge(scored[1], done(t.shift(-2)))
                        hold(pool)
                    pool.tensor_tensor(qk[:, t.u % 2, :, :], qk_parts[:, 0:2, :], qk_parts[:, 2:4, :], ALU.add)\
                        .then_inc(qk_copied, 1)

                def spread_keys(t):
                    p = t.u % 2
                    pool.wait_ge(qk_copied, done(t))
                    hold(pool)
                    if t.shift(-2).exists:
                        pool.wait_ge(scored[1], done(t.shift(-2)))
                        hold(pool)
                    lanes = net.headmask[:, :].rearrange("p (h o) -> p h o", o=1)
                    pool.tensor_tensor(k_blocks[:, p, :, :], qk[:, p, 1:2, :].to_broadcast([128, 8, TILE]),
                                       lanes.to_broadcast([128, 8, TILE]), ALU.mult).then_inc(spread, 1)

                def prepare(t):
                    p = t.u % 2
                    if mask_tile is not None:
                        pool.wait_ge(loaded[t.u % 2], landed(t, n_loads))
                        hold(pool)
                        if t.shift(-2).exists:
                            pool.wait_ge(bounded_s, done(t.shift(-2), 2))
                            hold(pool)
                        if mask[1] == "keys":
                            pool.tensor_scalar(mask_one[:, p, :], mask_in[:, p, :], 0.0, -3.3e38, ALU.is_gt, ALU.mult)\
                                .then_inc(mask_step, 1)
                            pool.wait_ge(mask_step, done(t, 1, 2))
                            hold(pool)
                            pool.tensor_scalar(mask_tile[:, p, :], mask_one[:, p, :], BIG, None, ALU.add)\
                                .then_inc(mask_ready, 1)
                        else:
                            pool.tensor_scalar(mask_tile[:, p, :], mask_in[:, p, :], BIG, -1e9 / scale, ALU.mult, ALU.add)\
                                .then_inc(mask_ready, 1)

                def bias_residual(t):
                    p = t.u % 2
                    if row is not None:
                        pool.wait_ge(x_loaded[t.u % 2], landed(t))
                        hold(pool)
                        if t.shift(-2).exists:
                            pool.wait_ge(tail.summed, done(t.shift(-2)))
                            hold(pool)
                        pool.tensor_tensor(x_res[:, p, :], x_in[:, p, :], add_row[:, :], ALU.add).then_inc(biased, 1)

                def rms(t):
                    if lambdas is None:
                        return
                    keep = (1.0 - LAMBDA_INIT) ** 2
                    pool.wait_ge(o_steps, done(t, O_STEPS))
                    hold(pool)
                    pool.tensor_scalar(ms_eps[:, :], ms[:, :], 1.0 / (dv * keep), 1e-5 / keep, ALU.mult, ALU.add)\
                        .then_inc(ms_eps_done, 1)
                    pool.wait_ge(ms_eps_done, done(t))
                    hold(pool)
                    if t.shift(-1).exists:
                        pool.wait_ge(o_ready, done(t.shift(-1)))
                        hold(pool)
                    pool.tensor_tensor(rms_inv[:, :], ms_eps[:, :], net.minus_half[:, :], ALU.pow).then_inc(rms_done, 1)

                def turn(t):
                    if t.shift(-SUM).inside(TILES) and wo is not None:
                        tail.inverse_std(pool, t.shift(-SUM))
                    if t.shift(1 - SUM).inside(TILES):
                        bias_residual(t.shift(1 - SUM))
                    if t.shift(2).inside(TILES):
                        if rope:
                            add_rope(t.shift(2))
                        spread_keys(t.shift(2))
                        prepare(t.shift(2))
                    rms(t)
                    if wo is None:
                        tail.inverse_std(pool, t)

                for n in range(2):
                    t = end.shift(n - TILES)
                    if rope:
                        add_rope(t)
                    spread_keys(t)
                    prepare(t)
                    if n < 1 - SUM:
                        bias_residual(t)
                tile_loop(pool, turn)
                if wo is not None:
                    for k in range(SUM):
                        if k < SUM - 1:
                            bias_residual(end.shift(k + 1 - SUM))
                        tail.inverse_std(pool, end.shift(k - SUM))


class Sublayer:

    def __init__(self, net, ctx, name):
        self.net, self.nc, self.ctx, self.name = net, net.nc, ctx, name
        self.weights = self.sem("weights_loaded")
        self.loads = []

    def sb(self, what, shape, dt=F32):
        return self.ctx.enter_context(self.nc.sbuf_tensor(f"{self.name}_{what}", shape, dt))

    def sem(self, what):
        return self.net.semaphore(f"{self.name}_{what}")

    def bank(self, what):
        return self.ctx.enter_context(self.nc.psum_tensor(f"{self.name}_{what}", [128, 512], F32))

    def load(self, what, shape, src, view=None):
        t = self.sb(what, shape)
        self.loads.append((view(t) if view else t[tuple(slice(None) for _ in shape)], src))
        return t

    def row(self, what, src, n):
        return self.load(what, [128, n], src.rearrange("(o n) -> o n", o=1).to_broadcast([128, n]))

    def start_loads(self, eng):
        for dst, src in self.loads:
            with self.nc.allow_non_contiguous_dma(reason="weights, once"):
                eng.dma_start(dst, src).then_inc(self.weights, 16)

    def await_weights(self, eng):
        eng.wait_ge(self.weights, 16 * len(self.loads))


class ChunkInput:

    def __init__(self, sub, cross=False):
        self.sub, self.net = sub, sub.net
        self.x = sub.sb("x_in", [128, 2, PER, D])
        self.xT = sub.sb("xT_in", [128, 2, CHUNK])
        self.cT = sub.sb("cT_in", [128, 2, CHUNK]) if cross else None
        self.loaded = [sub.sem("chunk_loaded_even"), sub.sem("chunk_loaded_odd")]
        self.dmas = 3 if cross else 2

    def load(self, sp, c, used):
        p = c.u % 2
        for s, times in used:
            if c.shift(-2).exists:
                sp.wait_ge(s, done(c.shift(-2), times))
                hold(sp)
        sp.dma_start(self.x[:, p, :, :], self.net.x_tok[:, bass.ds(c.n * PER, PER), :]).then_inc(self.loaded[p], 16)
        sp.dma_start(self.xT[:, p, :], self.net.x_T[:, tile_cols(c, CHUNK)]).then_inc(self.loaded[p], 16)
        if self.cT is not None:
            sp.dma_start(self.cT[:, p, :], self.net.dram["ctx_T"][:, tile_cols(c, CHUNK)]).then_inc(self.loaded[p], 16)

    def arrived(self, eng, c):
        eng.wait_ge(self.loaded[c.u % 2], landed(c, self.dmas))


class ChunkTail:

    def __init__(self, sub, final, summed=None):
        self.net, self.final = sub.net, final
        sb, sem = sub.sb, sub.sem
        self.r = sb("resid_sum", [128, 2, PER, D])
        self.stats = sb("ln_stats", [128, PER, 6])
        self.mv = sb("ln_moments", [128, 2, PER, 2])
        self.ve = sb("ln_var_eps", [128, PER])
        self.rstd = sb("ln_rstd", [128, 2, PER])
        self.xn = sb("ln_out", [128, 2, PER, D])
        self.xT = sb("ln_out_T", [128, 2, CHUNK])
        self.summed, self.sums = summed if summed else (sem("resid_summed"), 1)
        self.stats_done = sem("ln_stats_done")
        self.moments_done = sem("ln_moments_done")
        self.ve_done = sem("ln_var_eps_done")
        self.rstd_done = sem("ln_rstd_done")
        self.normed = sem("ln_normed")
        self.xT_ready = sem("ln_out_transposed")
        self.xT_copied = sem("ln_out_T_copied")
        self.stored = [sem("ln_stored_even"), sem("ln_stored_odd")]
        self.stores = 1 if final else 2

    def moments(self, dve, c):
        p = c.u % 2
        dve.wait_ge(self.summed, done(c, self.sums))
        for k in range(PER):
            last = dve.bn_stats(self.stats[:, k, :], self.r[:, p, k, :])
        last.then_inc(self.stats_done, 1)
        dve.wait_ge(self.stats_done, done(c))
        hold(dve)
        for k in range(PER):
            last = dve.bn_aggr(self.mv[:, p, k, :], self.stats[:, k, :])
        last.then_inc(self.moments_done, 1)

    def inverse_std(self, pool, c):
        p = c.u % 2
        pool.wait_ge(self.moments_done, done(c))
        hold(pool)
        pool.tensor_scalar(self.ve[:, :], self.mv[:, p, :, 1], LN_EPS, None, ALU.add).then_inc(self.ve_done, 1)
        pool.wait_ge(self.ve_done, done(c))
        hold(pool)
        pool.tensor_tensor(self.rstd[:, p, :], self.ve[:, :], self.net.minus_half[:, 0:PER], ALU.pow)\
            .then_inc(self.rstd_done, 1)

    def normalise(self, dve, c):
        p = c.u % 2
        dve.wait_ge(self.rstd_done, done(c))
        if c.shift(-2).exists:
            dve.wait_ge(self.stored[c.shift(-2).u % 2], landed(c.shift(-2), self.stores))
        if not self.final:
            if c.shift(-2).exists:
                dve.wait_ge(self.xT_ready, done(c.shift(-2)))
        for k in range(PER):
            last = dve.tensor_scalar(self.xn[:, p, k, :], self.r[:, p, k, :], self.mv[:, p, k, 0:1],
                                     self.rstd[:, p, k:k + 1], ALU.subtract, ALU.mult)
        last.then_inc(self.normed, 1)

    def transpose(self, pe, c, bank):
        if self.final:
            return
        pe.wait_ge(self.normed, done(c))
        if c.shift(-1).exists:
            pe.wait_ge(self.xT_copied, done(c.shift(-1)))
        for k in range(PER):
            last = pe.transpose(bank[:, TILE * k:TILE * k + TILE], self.xn[:, c.u % 2, k, :], self.net.ident[:, :])
        last.then_inc(self.xT_ready, 1)

    def copy_transposed(self, act, c, bank):
        if self.final:
            return
        act.wait_ge(self.xT_ready, done(c))
        if c.shift(-2).exists:
            act.wait_ge(self.stored[c.shift(-2).u % 2], landed(c.shift(-2), self.stores))
        act.activation(self.xT[:, c.u % 2, :], bank[:, :], ACT.Copy).then_inc(self.xT_copied, 1)

    def store(self, sp, c):
        p = c.u % 2
        sp.wait_ge(self.normed, done(c))
        hold(sp)
        if self.final:
            out = self.net.dram["out"].rearrange("(t p) d -> p t d", p=TILE)
            sp.dma_start(out[:, bass.ds(c.n * PER, PER), :], self.xn[:, p, :, :]).then_inc(self.stored[p], 16)
            return
        sp.dma_start(self.net.x_tok[:, bass.ds(c.n * PER, PER), :], self.xn[:, p, :, :]).then_inc(self.stored[p], 16)
        sp.wait_ge(self.xT_copied, done(c))
        hold(sp)
        sp.dma_start(self.net.x_T[:, tile_cols(c, CHUNK)], self.xT[:, p, :]).then_inc(self.stored[p], 16)

    def all_stored(self, sp):
        for p in range(2):
            sp.wait_ge(self.stored[p], 16 * self.stores * CHUNKS // 2)


def first_chunks():
    return Step(0, 0, 2), Step(0, 1, 2)


def last_chunk():
    return Step(CHUNKS // 2, 0, 2).shift(-1)


def chunk_loop(eng, body):
    def turn(i):
        for u in range(2):
            body(Step(i, u, 2))
    run_loop(eng, 2, CHUNKS, turn)


def stream(sub, block, inp, tail, used, early=False):
    @block.sync
    def _(sp):
        sub.start_loads(sp)
        for c in first_chunks():
            inp.load(sp, c, used)

        def body(c):
            if early and c.shift(2).inside(CHUNKS):
                inp.load(sp, c.shift(2), used)
            if c.shift(-1).inside(CHUNKS):
                tail.store(sp, c.shift(-1))
            if not early and c.shift(2).inside(CHUNKS):
                inp.load(sp, c.shift(2), used)

        chunk_loop(sp, body)
        tail.store(sp, last_chunk())
        tail.all_stored(sp)


def per_tile(x):
    return x.rearrange("p (k n) -> p k n", k=PER)


def spread_last(x, n):
    return x.rearrange("p (k o) -> p k o", o=1).to_broadcast([x.shape[0], x.shape[1], n])


class Router:

    RANKED, TWO = 5, 7

    def __init__(self, sub, E):
        sb, self.steps = sub.sb, sub.sem("router_steps")
        self.E = E
        self.iota = sub.load("iota", [128, E], sub.net.dram["c_iota"][:, 0:E])
        self.logits = sb("logits", [128, PER, E])
        self.top8, self.index8 = sb("top8", [128, PER, 8]), sb("index8", [128, PER, 8], U32)
        self.index = sb("index", [128, PER, 2])
        self.shifted = sb("shifted", [128, PER, E])
        self.exps = sb("exps", [128, PER, E])
        self.hot = sb("hot", [128, 2, PER, E])
        self.second, self.both = sb("second", [128, PER, E]), sb("both", [128, PER, E])
        self.total, self.weight = sb("total", [128, PER]), sb("weight", [128, PER])

    def rank(self, dve, steps, got, bias=None):
        if bias is not None:
            dve.tensor_tensor(self.logits[:, :, :], got, bias.rearrange("p (o e) -> p o e", o=1)
                              .to_broadcast([128, PER, self.E]), ALU.add).then_inc(self.steps, 1)
            dve.wait_ge(self.steps, steps.next())
            hold(dve)
        else:
            dve.tensor_copy(self.logits[:, :, :], got).then_inc(self.steps, 1)
            dve.wait_ge(self.steps, steps.next())
            hold(dve)
        for k in range(PER):
            last = dve.max(self.top8[:, k, :], self.logits[:, k, :])
        last.then_inc(self.steps, 1)
        dve.wait_ge(self.steps, steps.next())
        hold(dve)
        for k in range(PER):
            last = dve.max_index(self.index8[:, k, :], self.top8[:, k, :], self.logits[:, k, :])
        last.then_inc(self.steps, 1)
        dve.wait_ge(self.steps, steps.next())
        hold(dve)
        dve.tensor_copy(self.index[:, :, :], self.index8[:, :, 0:2]).then_inc(self.steps, 1)
        dve.wait_ge(self.steps, steps.next())
        hold(dve)
        dve.tensor_tensor(self.shifted[:, :, :], self.logits[:, :, :],
                          self.top8[:, :, 0:1].to_broadcast([128, PER, self.E]), ALU.subtract).then_inc(self.steps, 1)
        dve.wait_ge(self.steps, steps.next())
        hold(dve)

    def one_hot(self, dve, steps, r):
        ids = self.iota[:, :].rearrange("p (o e) -> p o e", o=1).to_broadcast([128, PER, self.E])
        dve.tensor_tensor(self.hot[:, r, :, :], ids, self.index[:, :, r:r + 1].to_broadcast([128, PER, self.E]),
                          ALU.is_equal).then_inc(self.steps, 1)
        dve.wait_ge(self.steps, steps.next())
        hold(dve)

    def mix_two(self, dve, steps, out, wait_exps):
        for r in range(2):
            self.one_hot(dve, steps, r)
        wait_exps()
        dve.tensor_tensor(self.second[:, :, :], self.exps[:, :, :], self.hot[:, 1, :, :], ALU.mult).then_inc(self.steps, 1)
        dve.wait_ge(self.steps, steps.next())
        hold(dve)
        dve.tensor_tensor(self.both[:, :, :], self.second[:, :, :], self.hot[:, 0, :, :], ALU.add).then_inc(self.steps, 1)
        dve.wait_ge(self.steps, steps.next())
        hold(dve)
        dve.tensor_reduce(self.total[:, :], self.both[:, :, :], AX_X, ALU.add).then_inc(self.steps, 1)
        dve.wait_ge(self.steps, steps.next())
        hold(dve)
        dve.reciprocal(self.weight[:, :], self.total[:, :]).then_inc(self.steps, 1)
        dve.wait_ge(self.steps, steps.next())
        hold(dve)
        dve.tensor_tensor(out, self.both[:, :, :], spread_last(self.weight[:, :], self.E), ALU.mult).then_inc(self.steps, 1)
        dve.wait_ge(self.steps, steps.next())
        hold(dve)


def moe(net, final, name, gate_w, w1, b1, w2, b2, gelu, gate_b=None, top=1):
    nc, dram = net.nc, net.dram
    E = EXPERTS
    with ExitStack() as ctx:
        sub = Sublayer(net, ctx, name)
        sb, sem, bank = sub.sb, sub.sem, sub.bank
        gate_s = sub.load("gate_w", [128, E], gate_w)
        w1_s = sub.load("w1", [128, E, FF], w1.rearrange("e d f -> d e f"))
        w2_s = sub.load("w2", [128, E * FB, D], w2.rearrange("e (b p) d -> p (e b) d", p=128))
        b1_s = sub.load("b1", [128, E * FB], b1)
        b2_s = sub.load("b2", [E, D], b2)
        router = Router(sub, E)
        gate_b_s = sub.row("gate_b", gate_b, E) if gate_b is not None else None
        if top == 1:
            before = sub.load("before", [128, 128], dram["c_before"])
            run = sb("tokens_so_far", [128, PER + 1, E])
            counts = sb("counts", [128, PER, E])
            rank, valid = sb("rank", [128, PER]), sb("valid", [128, PER])
        exps, hot, total, weight = router.exps, router.hot, router.total, router.weight
        mix = sb("mix", [128, 2, PER, E])
        mix_T = sb("mix_T", [E, CHUNK])
        hid = sb("hid", [128, 2, FB, CHUNK])
        acc = sb("acc", [128, PER, D])
        inp = ChunkInput(sub)

        hid_bank = [bank("hid0"), bank("hid1")]
        out_bank = [bank("out0"), bank("out1")]
        route_bank = bank("route")
        mixT_bank = bank("mixT")
        bias_bank = bank("bias")
        xT_bank = bank("xT")

        routed, counted = sem("logits_ready"), sem("counts_ready")
        hid_ready, hid_done = sem("hid_ready"), sem("hid_done")
        out_ready, out_added = sem("out_ready"), sem("out_added")
        mixT_ready, mixT_copied = sem("mixT_ready"), sem("mixT_copied")
        bias_ready, exp_done = sem("bias_ready"), sem("exp_done")
        started, run_cleared = sem("acc_started"), sem("run_cleared")
        r_steps = router.steps
        tail = ChunkTail(sub, final, (out_added, E))
        SHIFTED, RUN, MIXED = (5, 11, 17) if top == 1 else (5, None, 12)
        R = MIXED

        with nc.Block() as block:
            stream(sub, block, inp, tail, [(started, 1), (hid_ready, E * FB)])

            @block.tensor
            def _(pe):
                sub.await_weights(pe)

                def hidden(c, e):
                    for b in range(FB):
                        q = (e * FB + b) % 2
                        if e * FB + b >= 2:
                            pe.wait_ge(hid_done, nth(c, E * FB, e * FB + b - 1))
                        elif c.shift(-1).exists:
                            pe.wait_ge(hid_done, done(c.shift(-1), E * FB, e * FB + b - 1))
                        pe.matmul(hid_bank[q][:, :], w1_s[:, e, 128 * b:128 * b + 128], inp.xT[:, c.u % 2, :],
                                  start=True, stop=True).then_inc(hid_ready, 1)

                def output(c, e):
                    pe.wait_ge(hid_done, nth(c, E * FB, (e + 1) * FB))
                    if e >= 2:
                        pe.wait_ge(out_added, nth(c, E, e - 1))
                    else:
                        if c.shift(-1).exists:
                            pe.wait_ge(out_added, nth(c.shift(-1), E, E + e - 1))
                    for k in range(PER):
                        for b in range(FB):
                            last = pe.matmul(out_bank[e % 2][:, D * k:D * k + D], hid[:, e % 2, b, TILE * k:TILE * k + TILE],
                                             w2_s[:, e * FB + b, :], start=(b == 0), stop=(b == FB - 1))
                    last.then_inc(out_ready, 1)

                def logits(c):
                    pe.wait_ge(inp.loaded[c.u % 2], landed(c, inp.dmas))
                    if c.shift(-1).exists:
                        pe.wait_ge(r_steps, nth(c.shift(-1), R, R))
                    for k in range(PER):
                        last = pe.matmul(route_bank[:, E * k:E * k + E], inp.xT[:, c.u % 2, TILE * k:TILE * k + TILE],
                                         gate_s[:, :], start=True, stop=True)
                    last.then_inc(routed, 1)

                def count(c):
                    if top == 2:
                        return
                    pe.wait_ge(r_steps, nth(c, R, RUN))
                    for k in range(PER):
                        pe.matmul(route_bank[:, 64 + E * k:64 + E * k + E], before[:, :], hot[:, 0, k, :],
                                  start=True, stop=False)
                        last = pe.matmul(route_bank[:, 64 + E * k:64 + E * k + E], net.ones[:, :], run[:, k, :],
                                         start=False, stop=True)
                    last.then_inc(counted, 1)

                def transpose_mix(c):
                    pe.wait_ge(r_steps, nth(c, R, MIXED))
                    if c.shift(-1).exists:
                        pe.wait_ge(mixT_copied, done(c.shift(-1)))
                    for k in range(PER):
                        last = pe.transpose(mixT_bank[0:E, TILE * k:TILE * k + TILE], mix[:, c.u % 2, k, :],
                                            net.ident[:, :])
                    last.then_inc(mixT_ready, 1)

                def biases(c):
                    pe.wait_ge(mixT_copied, done(c))
                    if c.shift(-1).exists:
                        pe.wait_ge(started, done(c.shift(-1)))
                    for k in range(PER):
                        last = pe.matmul(bias_bank[:, D * k:D * k + D], mix_T[:, TILE * k:TILE * k + TILE], b2_s[:, :],
                                         start=True, stop=True)
                    last.then_inc(bias_ready, 1)

                ahead = {2: logits, 4: count, 5: transpose_mix, 6: biases}

                def body(c):
                    hidden(c, 0)
                    for e in range(1, E):
                        hidden(c, e)
                        if e in ahead and c.shift(1).inside(CHUNKS):
                            ahead[e](c.shift(1))
                        output(c, e - 1)
                        if e == 2 and c.shift(-1).inside(CHUNKS):
                            tail.transpose(pe, c.shift(-1), xT_bank)
                    output(c, E - 1)

                for stage in ahead.values():
                    stage(first_chunks()[0])
                chunk_loop(pe, body)
                tail.transpose(pe, last_chunk(), xT_bank)

            @block.scalar
            def _(act):
                sub.await_weights(act)

                def activate(c, e):
                    for b in range(FB):
                        n = e * FB + b
                        act.wait_ge(hid_ready, nth(c, E * FB, n + 1))
                        if e >= 2:
                            act.wait_ge(out_ready, nth(c, E, e - 1))
                        else:
                            if c.shift(-1).exists:
                                act.wait_ge(out_ready, nth(c.shift(-1), E, E + e - 1))
                        act.activation(hid[:, e % 2, b, :], hid_bank[n % 2][:, :], gelu, bias=b1_s[:, n:n + 1])\
                            .then_inc(hid_done, 1)

                def exponentials(c):
                    act.wait_ge(r_steps, nth(c, R, SHIFTED))
                    act.activation(exps[:, :, :], router.shifted[:, :, :], ACT.Exp).then_inc(exp_done, 1)

                def copy_mix(c):
                    act.wait_ge(mixT_ready, done(c))
                    if c.shift(-1).exists:
                        act.wait_ge(bias_ready, done(c.shift(-1)))
                    act.activation(mix_T[:, :], mixT_bank[0:E, :], ACT.Copy).then_inc(mixT_copied, 1)

                def body(c):
                    for e in range(E):
                        activate(c, e)
                        if e == 2 and c.shift(-1).inside(CHUNKS):
                            tail.copy_transposed(act, c.shift(-1), xT_bank)
                        if e == 3 and c.shift(1).inside(CHUNKS):
                            exponentials(c.shift(1))
                        if e == 5 and c.shift(1).inside(CHUNKS):
                            copy_mix(c.shift(1))

                exponentials(first_chunks()[0])
                copy_mix(first_chunks()[0])
                chunk_loop(act, body)
                tail.copy_transposed(act, last_chunk(), xT_bank)

            @block.vector
            def _(dve):
                sub.await_weights(dve)
                if top == 1:
                    dve.memset(run[:, :, :], 0.0).then_inc(run_cleared, 1)
                    dve.wait_ge(run_cleared, 1)

                def choose(c, steps):
                    dve.wait_ge(routed, done(c))
                    got = route_bank[:, 0:PER * E].rearrange("p (k e) -> p k e", k=PER)
                    if c.shift(-1).exists:
                        dve.wait_ge(exp_done, done(c.shift(-1)))
                    router.rank(dve, steps, got, gate_b_s[:, :] if gate_b_s is not None else None)
                    if top == 2:
                        return
                    router.one_hot(dve, steps, 0)
                    dve.tensor_copy(run[:, 0, :], run[:, PER, :]).then_inc(r_steps, 1)
                    dve.wait_ge(r_steps, steps.next())
                    hold(dve)
                    for k in range(PER):
                        dve.tensor_tensor(run[:, k + 1, :], run[:, k, :], hot[:, 0, k, :], ALU.add)\
                            .then_inc(r_steps, 1)
                        dve.wait_ge(r_steps, steps.next())
                        hold(dve)

                def weigh(c, steps):
                    p = c.u % 2
                    if top == 2:
                        router.mix_two(dve, steps, mix[:, p, :, :], lambda: dve.wait_ge(exp_done, done(c)))
                        return
                    dve.wait_ge(exp_done, done(c))
                    dve.tensor_reduce(total[:, :], exps[:, :, :], AX_X, ALU.add).then_inc(r_steps, 1)
                    dve.wait_ge(r_steps, steps.next())
                    hold(dve)
                    dve.reciprocal(weight[:, :], total[:, :]).then_inc(r_steps, 1)
                    dve.wait_ge(r_steps, steps.next())
                    hold(dve)
                    dve.wait_ge(counted, done(c))
                    dve.tensor_tensor(counts[:, :, :], route_bank[:, 64:64 + PER * E]
                                      .rearrange("p (k e) -> p k e", k=PER), hot[:, 0, :, :], ALU.mult)\
                        .then_inc(r_steps, 1)
                    dve.wait_ge(r_steps, steps.next())
                    hold(dve)
                    dve.tensor_reduce(rank[:, :], counts[:, :, :], AX_X, ALU.add).then_inc(r_steps, 1)
                    dve.wait_ge(r_steps, steps.next())
                    hold(dve)
                    dve.scalar_tensor_tensor(valid[:, :], rank[:, :], float(CAPACITY), weight[:, :],
                                             ALU.is_le, ALU.mult).then_inc(r_steps, 1)
                    dve.wait_ge(r_steps, steps.next())
                    hold(dve)
                    dve.tensor_tensor(mix[:, p, :, :], hot[:, 0, :, :], spread_last(valid[:, :], E), ALU.mult)\
                        .then_inc(r_steps, 1)
                    dve.wait_ge(r_steps, steps.next())
                    hold(dve)

                def add(c, e):
                    p = c.u % 2
                    dve.wait_ge(out_ready, nth(c, E, e + 1))
                    if e == 0:
                        dve.wait_ge(started, done(c))
                    else:
                        dve.wait_ge(out_added, nth(c, E, e))
                    for k in range(PER):
                        dst = acc[:, k, :] if e < E - 1 else tail.r[:, p, k, :]
                        last = dve.scalar_tensor_tensor(dst, out_bank[e % 2][:, D * k:D * k + D], mix[:, p, k, e:e + 1],
                                                        acc[:, k, :], ALU.mult, ALU.add)
                    last.then_inc(out_added, 1)

                def body(c):
                    p = c.u % 2
                    dve.wait_ge(inp.loaded[c.u % 2], landed(c, inp.dmas))
                    dve.wait_ge(bias_ready, done(c))
                    dve.tensor_tensor(acc[:, :, :], per_tile(bias_bank[:, :]), inp.x[:, p, :, :], ALU.add)\
                        .then_inc(started, 1)
                    steps = StepCount(c.shift(1), R)
                    for e in range(E):
                        add(c, e)
                        if e == 0 and c.shift(-1).inside(CHUNKS):
                            tail.normalise(dve, c.shift(-1))
                        if e == 1 and c.shift(1).inside(CHUNKS):
                            choose(c.shift(1), steps)
                        if e == 3 and c.shift(1).inside(CHUNKS):
                            weigh(c.shift(1), steps)
                    tail.moments(dve, c)

                first = first_chunks()[0]
                steps = StepCount(first, R)
                choose(first, steps)
                weigh(first, steps)
                chunk_loop(dve, body)
                tail.normalise(dve, last_chunk())

            @block.gpsimd
            def _(pool):
                chunk_loop(pool, lambda c: tail.inverse_std(pool, c))


def ternary_ffn(net, final, name):
    nc, dram = net.nc, net.dram
    with ExitStack() as ctx:
        sub = Sublayer(net, ctx, name)
        sb, sem, bank = sub.sb, sub.sem, sub.bank
        w_s = [sub.load("w1", [128, FF], dram[f"{name}_W1T"]),
               sub.load("w2", [128, FB, D], dram[f"{name}_W2T"].rearrange("(b p) d -> p b d", p=128))]
        b1_s = sub.load("b1", [128, FB], dram[f"{name}_b1"])
        b2_s = sub.row("b2", dram[f"{name}_b2"], D)
        tern = [sb("tern1", [128, FF]), sb("tern2", [128, FF])]
        above, below, step = sb("above", [128, FF]), sb("below", [128, FF]), sb("step", [128, FF])
        lane_sum, mean, half = sb("lane_sum", [128, 2]), sb("mean", [128, 2]), sb("half", [128, 2, 2])
        hid = sb("hid", [128, 2, FB, CHUNK])
        x_res = sb("x_res", [128, 2, PER, D])
        inp, tail = ChunkInput(sub), ChunkTail(sub, final)
        hid_bank = [bank(f"hid{k}") for k in range(4)]
        y_bank = [bank("y0"), bank("y1")]
        xT_bank = bank("xT")
        sum_bank = bank("sum")
        prep, sums_ready, tern_ready = sem("prep_steps"), sem("sums_ready"), sem("weights_ternary")
        hid_ready, hid_done, y_ready, biased = sem("hid_ready"), sem("hid_done"), sem("y_ready"), sem("biased")
        with nc.Block() as block:
            stream(sub, block, inp, tail, [(biased, 1), (y_ready, 1)])

            @block.tensor
            def _(pe):
                pe.wait_ge(prep, 2)
                pe.matmul(sum_bank[:, 0:2], net.ones[:, :], lane_sum[:, :], start=True, stop=True).then_inc(sums_ready, 1)
                pe.wait_ge(tern_ready, 1)

                def hidden(c):
                    pe.wait_ge(inp.loaded[c.u % 2], landed(c, inp.dmas))
                    for b in range(FB):
                        if c.shift(-1).exists:
                            pe.wait_ge(hid_done, nth(c.shift(-1), FB, b + 1))
                        pe.matmul(hid_bank[b][:, :], tern[0][:, 128 * b:128 * b + 128], inp.xT[:, c.u % 2, :],
                                  start=True, stop=True).then_inc(hid_ready, 1)

                def body(c):
                    p = c.u % 2
                    if c.shift(1).inside(CHUNKS):
                        hidden(c.shift(1))
                    pe.wait_ge(hid_done, done(c, FB))
                    if c.shift(-2).exists:
                        pe.wait_ge(tail.summed, done(c.shift(-2)))
                    for k in range(PER):
                        for b in range(FB):
                            last = pe.matmul(y_bank[p][:, D * k:D * k + D], hid[:, p, b, TILE * k:TILE * k + TILE],
                                             tern[1][:, D * b:D * b + D], start=(b == 0), stop=(b == FB - 1))
                    last.then_inc(y_ready, 1)
                    if c.shift(-1).inside(CHUNKS):
                        tail.transpose(pe, c.shift(-1), xT_bank)

                hidden(first_chunks()[0])
                chunk_loop(pe, body)
                tail.transpose(pe, last_chunk(), xT_bank)

            @block.scalar
            def _(act):
                sub.await_weights(act)

                def body(c):
                    for b in range(FB):
                        act.wait_ge(hid_ready, nth(c, FB, b + 1))
                        if c.shift(-2).exists:
                            act.wait_ge(y_ready, done(c.shift(-2)))
                        act.activation(hid[:, c.u % 2, b, :], hid_bank[b][:, :], ACT.Gelu, bias=b1_s[:, b:b + 1])\
                            .then_inc(hid_done, 1)
                    if c.shift(-2).inside(CHUNKS):
                        tail.copy_transposed(act, c.shift(-2), xT_bank)

                chunk_loop(act, body)
                tail.copy_transposed(act, last_chunk().shift(-1), xT_bank)
                tail.copy_transposed(act, last_chunk(), xT_bank)

            @block.vector
            def _(dve):
                sub.await_weights(dve)
                steps = StepCount(Step(0, 0, 2), 15)
                flat = [w_s[0][:, :], w_s[1][:, :, :].rearrange("p b d -> p (b d)")]
                for r in range(2):
                    dve.tensor_reduce(lane_sum[:, r:r + 1], flat[r], AX_X, ALU.add, apply_absolute_value=True)\
                        .then_inc(prep, 1)
                    dve.wait_ge(prep, steps.next())
                    hold(dve)
                dve.wait_ge(sums_ready, 1)
                dve.tensor_scalar(mean[:, :], sum_bank[:, 0:2], 1.0 / (FF * D), 1e-8, ALU.mult, ALU.max)\
                    .then_inc(prep, 1)
                dve.wait_ge(prep, steps.next())
                hold(dve)
                dve.tensor_scalar(half[:, :, 0], mean[:, :], 0.5, None, ALU.mult).then_inc(prep, 1)
                dve.wait_ge(prep, steps.next())
                hold(dve)
                dve.tensor_scalar(half[:, :, 1], mean[:, :], -0.5, None, ALU.mult).then_inc(prep, 1)
                dve.wait_ge(prep, steps.next())
                hold(dve)
                for r in range(2):
                    dve.tensor_scalar(above[:, :], flat[r], half[:, r, 0:1], None, ALU.is_gt).then_inc(prep, 1)
                    dve.wait_ge(prep, steps.next())
                    hold(dve)
                    dve.tensor_scalar(below[:, :], flat[r], half[:, r, 1:2], None, ALU.is_lt).then_inc(prep, 1)
                    dve.wait_ge(prep, steps.next())
                    hold(dve)
                    dve.tensor_tensor(step[:, :], above[:, :], below[:, :], ALU.subtract).then_inc(prep, 1)
                    dve.wait_ge(prep, steps.next())
                    hold(dve)
                    dve.tensor_tensor(above[:, :], step[:, :], flat[r], ALU.subtract).then_inc(prep, 1)
                    dve.wait_ge(prep, steps.next())
                    hold(dve)
                    dve.tensor_tensor(tern[r][:, :], above[:, :], flat[r], ALU.add).then_inc(prep, 1)
                    dve.wait_ge(prep, steps.next())
                    hold(dve)
                dve.memset(step[:, 0:1], 0.0).then_inc(tern_ready, 1)

                def body(c):
                    p = c.u % 2
                    dve.wait_ge(y_ready, done(c))
                    dve.wait_ge(biased, done(c))
                    if c.shift(-2).exists:
                        dve.wait_ge(tail.normed, done(c.shift(-2)))
                    dve.tensor_tensor(tail.r[:, p, :, :], per_tile(y_bank[p][:, :]), x_res[:, p, :, :], ALU.add)\
                        .then_inc(tail.summed, 1)
                    tail.moments(dve, c)
                    tail.normalise(dve, c)

                chunk_loop(dve, body)

            @block.gpsimd
            def _(pool):
                sub.await_weights(pool)

                def body(c):
                    p = c.u % 2
                    pool.wait_ge(inp.loaded[c.u % 2], landed(c, inp.dmas))
                    hold(pool)
                    if c.shift(-2).exists:
                        pool.wait_ge(tail.summed, done(c.shift(-2)))
                        hold(pool)
                    pool.tensor_tensor(x_res[:, p, :, :], inp.x[:, p, :, :], b2_s[:, :].rearrange("p (o d) -> p o d", o=1)
                                       .to_broadcast([128, PER, D]), ALU.add).then_inc(biased, 1)
                    tail.inverse_std(pool, c)

                chunk_loop(pool, body)


def moe_small(net, final, name):
    nc, dram = net.nc, net.dram
    E, KB = 32, 8
    with ExitStack() as ctx:
        sub = Sublayer(net, ctx, name)
        sb, sem, bank = sub.sb, sub.sem, sub.bank
        router_s = sub.load("router_w", [128, E], dram[f"{name}_router_wT"])
        router_b = sub.row("router_b", dram[f"{name}_router_b"], E)
        w1_s = sub.load("w1", [128, E * 32], dram[f"{name}_weights1"].rearrange("e d h -> d e h"),
                        lambda t: t[:, :].rearrange("p (e h) -> p e h", e=E))
        w2_s = sub.load("w2", [128, KB, D], dram[f"{name}_weights2"].rearrange("e h d -> (e h) d")
                        .rearrange("(b p) d -> p b d", p=128))
        b1_s = sub.load("b1", [128, KB], dram[f"{name}_bias1"])
        b2_s = sub.load("b2", [E, D], dram[f"{name}_bias2"])
        iota = sub.load("iota", [128, E], dram["c_iota"])
        select = sub.load("select", [E, E * 32], dram["c_esel"])
        logits = sb("logits", [128, PER, E])
        top8, index8, index = sb("top8", [128, PER, 8]), sb("index8", [128, PER, 8], U32), sb("index", [128, PER, 1])
        hot = sb("hot", [128, PER, E])
        hot_T = sb("hot_T", [E, CHUNK])
        select_bf, block_T = sb("select_bf", [E, E * 32], BF16), sb("block_T", [E, CHUNK], BF16)
        hid = sb("hid", [128, KB, CHUNK])
        inp, tail = ChunkInput(sub), ChunkTail(sub, final)
        hid_bank = [bank("hid0"), bank("hid1"), bank("hid2")]
        y_bank = [bank("y0"), bank("y1")]
        route_bank, hotT_bank, xT_bank = bank("route"), bank("hotT"), bank("xT")
        routed, r_steps, hotT_ready = sem("logits_ready"), sem("router_steps"), sem("hotT_ready")
        hid_ready, hid_done, y_ready = sem("hid_ready"), sem("hid_done"), sem("y_ready")
        select_cast = sem("select_cast")
        R = 7
        with nc.Block() as block:
            stream(sub, block, inp, tail, [(tail.summed, 1), (hid_ready, KB)])

            @block.tensor
            def _(pe):
                sub.await_weights(pe)

                def route(c):
                    pe.wait_ge(inp.loaded[c.u % 2], landed(c, inp.dmas))
                    if c.shift(-1).exists:
                        pe.wait_ge(r_steps, nth(c.shift(-1), R, 1))
                    for k in range(PER):
                        last = pe.matmul(route_bank[:, E * k:E * k + E], inp.xT[:, c.u % 2, TILE * k:TILE * k + TILE],
                                         router_s[:, :], start=True, stop=True)
                    last.then_inc(routed, 1)

                def transpose_hot(c):
                    pe.wait_ge(r_steps, nth(c, R, 5))
                    if c.shift(-1).exists:
                        pe.wait_ge(r_steps, nth(c.shift(-1), R, R))
                    for k in range(PER):
                        last = pe.transpose(hotT_bank[0:E, TILE * k:TILE * k + TILE], hot[:, k, :], net.ident[:, :])
                    last.then_inc(hotT_ready, 1)

                def body(c):
                    pe.wait_ge(r_steps, nth(c, R, R))
                    for b in range(KB):
                        if b >= 3:
                            pe.wait_ge(hid_done, nth(c, KB, b - 2))
                        else:
                            if c.shift(-1).exists:
                                pe.wait_ge(hid_done, nth(c.shift(-1), KB, KB + b - 2))
                        h = hid_bank[b % 3]
                        pe.matmul(h[:, :], w1_s[:, 128 * b:128 * b + 128], inp.xT[:, c.u % 2, :], start=True, stop=False)
                        pe.matmul(h[:, :], select_bf[:, 128 * b:128 * b + 128], block_T[:, :], start=False, stop=True)\
                            .then_inc(hid_ready, 1)
                    if c.shift(1).inside(CHUNKS):
                        route(c.shift(1))
                    if c.shift(-1).inside(CHUNKS):
                        tail.transpose(pe, c.shift(-1), xT_bank)
                    pe.wait_ge(hid_done, nth(c, KB, KB))
                    if c.shift(-2).exists:
                        pe.wait_ge(tail.summed, done(c.shift(-2)))
                    y = y_bank[c.u % 2]
                    for k in range(PER):
                        tok = slice(TILE * k, TILE * k + TILE)
                        for b in range(KB):
                            pe.matmul(y[:, D * k:D * k + D], hid[:, b, tok], w2_s[:, b, :], start=(b == 0), stop=False)
                        last = pe.matmul(y[:, D * k:D * k + D], hot_T[:, tok], b2_s[:, :], start=False, stop=True)
                    last.then_inc(y_ready, 1)
                    if c.shift(1).inside(CHUNKS):
                        transpose_hot(c.shift(1))

                pe.wait_ge(select_cast, 1)
                route(first_chunks()[0])
                transpose_hot(first_chunks()[0])
                chunk_loop(pe, body)
                tail.transpose(pe, last_chunk(), xT_bank)

            @block.scalar
            def _(act):
                sub.await_weights(act)

                def body(c):
                    for b in range(KB):
                        act.wait_ge(hid_ready, nth(c, KB, b + 1))
                        if c.shift(-1).exists:
                            act.wait_ge(y_ready, done(c.shift(-1)))
                        act.activation(hid[:, b, :], hid_bank[b % 3][:, :], ACT.Relu, bias=b1_s[:, b:b + 1])\
                            .then_inc(hid_done, 1)
                    if c.shift(-1).inside(CHUNKS):
                        tail.copy_transposed(act, c.shift(-1), xT_bank)

                chunk_loop(act, body)
                tail.copy_transposed(act, last_chunk(), xT_bank)

            @block.vector
            def _(dve):
                sub.await_weights(dve)
                dve.tensor_copy(select_bf[:, :], select[:, :]).then_inc(select_cast, 1)

                def route(c):
                    dve.wait_ge(routed, done(c))
                    steps = StepCount(c, R)
                    dve.tensor_tensor(logits[:, :, :], route_bank[:, 0:PER * E].rearrange("p (k e) -> p k e", k=PER),
                                      router_b[:, :].rearrange("p (o e) -> p o e", o=1).to_broadcast([128, PER, E]),
                                      ALU.add).then_inc(r_steps, 1)
                    dve.wait_ge(r_steps, steps.next())
                    hold(dve)
                    for k in range(PER):
                        last = dve.max(top8[:, k, :], logits[:, k, :])
                    last.then_inc(r_steps, 1)
                    dve.wait_ge(r_steps, steps.next())
                    hold(dve)
                    for k in range(PER):
                        last = dve.max_index(index8[:, k, :], top8[:, k, :], logits[:, k, :])
                    last.then_inc(r_steps, 1)
                    dve.wait_ge(r_steps, steps.next())
                    hold(dve)
                    dve.tensor_copy(index[:, :, :], index8[:, :, 0:1]).then_inc(r_steps, 1)
                    dve.wait_ge(r_steps, steps.next())
                    hold(dve)
                    dve.tensor_tensor(hot[:, :, :], iota[:, :].rearrange("p (o e) -> p o e", o=1)
                                      .to_broadcast([128, PER, E]), index[:, :, :].to_broadcast([128, PER, E]),
                                      ALU.is_equal).then_inc(r_steps, 1)
                    dve.wait_ge(r_steps, steps.next())
                    hold(dve)
                    dve.wait_ge(hotT_ready, done(c))
                    if c.shift(-1).exists:
                        dve.wait_ge(y_ready, done(c.shift(-1)))
                    dve.tensor_copy(hot_T[:, :], hotT_bank[0:E, :]).then_inc(r_steps, 1)
                    dve.wait_ge(r_steps, steps.next())
                    hold(dve)
                    dve.tensor_scalar(block_T[:, :], hotT_bank[0:E, :], 1.0, 1e30, ALU.subtract, ALU.mult)\
                        .then_inc(r_steps, 1)
                    dve.wait_ge(r_steps, steps.next())
                    hold(dve)

                def residual(c):
                    p = c.u % 2
                    dve.wait_ge(inp.loaded[c.u % 2], landed(c, inp.dmas))
                    dve.wait_ge(y_ready, done(c))
                    if c.shift(-2).exists:
                        dve.wait_ge(tail.normed, done(c.shift(-2)))
                    dve.scalar_tensor_tensor(tail.r[:, p, :, :].rearrange("p k d -> p (k d)"), y_bank[p][:, :], 0.0,
                                             inp.x[:, p, :, :].rearrange("p k d -> p (k d)"), ALU.max, ALU.add)\
                        .then_inc(tail.summed, 1)
                    tail.moments(dve, c)

                def body(c):
                    if c.shift(-1).inside(CHUNKS):
                        tail.normalise(dve, c.shift(-1))
                    if c.shift(1).inside(CHUNKS):
                        route(c.shift(1))
                    residual(c)

                route(first_chunks()[0])
                chunk_loop(dve, body)
                tail.normalise(dve, last_chunk())

            @block.gpsimd
            def _(pool):
                chunk_loop(pool, lambda c: tail.inverse_std(pool, c))


def gated_scan(net, final, name):
    nc, dram = net.nc, net.dram
    with ExitStack() as ctx:
        sub = Sublayer(net, ctx, name)
        sb, sem, bank = sub.sb, sub.sem, sub.bank
        w_s = sub.load("w", [128, 3 * D], dram[f"{name}_W_qkvaT"])
        gamma = sub.load("gamma", [128, 1], dram[f"{name}_gamma"].rearrange("(p o) -> p o", o=1))
        sq = sb("sq", [128, PER, D])
        ss, ss_max, inv = sb("ss", [128, PER]), sb("ss_max", [128, PER]), sb("inv", [128, PER])
        xs, xn_T = sb("xs", [128, PER, D]), sb("xn_T", [128, CHUNK])
        gate, h, out = sb("gate", [128, CHUNK]), sb("h", [128, CHUNK]), sb("out_T", [128, CHUNK])
        inp, tail = ChunkInput(sub), ChunkTail(sub, final)
        xs_bank, q_bank, kv_bank, a_bank = bank("xsT"), bank("q"), bank("kv"), bank("a")
        y_bank, xT_bank = bank("y"), bank("xT")
        n_steps, inverted = sem("norm_steps"), sem("inverted")
        xs_T, xs_copied, projected = sem("xsT_ready"), sem("xsT_copied"), sem("projected")
        gated, s_steps, y_ready = sem("gate_ready"), sem("scan_steps"), sem("y_ready")
        with nc.Block() as block:
            stream(sub, block, inp, tail, [(tail.summed, 1)])

            @block.tensor
            def _(pe):
                sub.await_weights(pe)

                def body(c):
                    pe.wait_ge(n_steps, nth(c, 4, 4))
                    if c.shift(-1).exists:
                        pe.wait_ge(xs_copied, done(c.shift(-1)))
                    for k in range(PER):
                        last = pe.transpose(xs_bank[:, TILE * k:TILE * k + TILE], xs[:, k, :], net.ident[:, :])
                    last.then_inc(xs_T, 1)
                    pe.wait_ge(xs_copied, done(c))
                    if c.shift(-1).exists:
                        pe.wait_ge(s_steps, nth(c.shift(-1), 3, 3))
                    for r, b in ((2, a_bank), (1, kv_bank), (0, q_bank)):
                        last = pe.matmul(b[:, :], w_s[:, D * r:D * r + D], xn_T[:, :], start=True, stop=True)
                    last.then_inc(projected, 1)
                    if c.shift(-1).inside(CHUNKS):
                        tail.transpose(pe, c.shift(-1), xT_bank)
                    pe.wait_ge(s_steps, nth(c, 3, 3))
                    if c.shift(-1).exists:
                        pe.wait_ge(tail.summed, done(c.shift(-1)))
                    for k in range(PER):
                        last = pe.transpose(y_bank[:, D * k:D * k + D], out[:, TILE * k:TILE * k + TILE], net.ident[:, :])
                    last.then_inc(y_ready, 1)

                chunk_loop(pe, body)
                tail.transpose(pe, last_chunk(), xT_bank)

            @block.scalar
            def _(act):
                sub.await_weights(act)

                def body(c):
                    act.wait_ge(xs_T, done(c))
                    if c.shift(-1).exists:
                        act.wait_ge(projected, done(c.shift(-1)))
                    act.activation(xn_T[:, :], xs_bank[:, :], ACT.Copy, scale=gamma[:, 0:1]).then_inc(xs_copied, 1)
                    if c.shift(-1).inside(CHUNKS):
                        tail.copy_transposed(act, c.shift(-1), xT_bank)
                    act.wait_ge(projected, done(c))
                    if c.shift(-1).exists:
                        act.wait_ge(s_steps, nth(c.shift(-1), 3, 2))
                    act.activation(gate[:, :], a_bank[:, :], ACT.Sigmoid).then_inc(gated, 1)

                chunk_loop(act, body)
                tail.copy_transposed(act, last_chunk(), xT_bank)

            @block.vector
            def _(dve):
                def body(c):
                    p = c.u % 2
                    x = inp.x[:, p, :, :]
                    dve.wait_ge(inp.loaded[c.u % 2], landed(c, inp.dmas))
                    steps = StepCount(c, 4)
                    dve.tensor_tensor(sq[:, :, :], x, x, ALU.mult).then_inc(n_steps, 1)
                    dve.wait_ge(n_steps, steps.next())
                    hold(dve)
                    dve.tensor_reduce(ss[:, :], sq[:, :, :], AX_X, ALU.add).then_inc(n_steps, 1)
                    dve.wait_ge(n_steps, steps.next())
                    hold(dve)
                    if c.shift(-1).exists:
                        dve.wait_ge(inverted, done(c.shift(-1)))
                    dve.tensor_scalar(ss_max[:, :], ss[:, :], 1e-24, None, ALU.max).then_inc(n_steps, 1)
                    dve.wait_ge(n_steps, steps.next())
                    hold(dve)
                    if c.shift(-1).inside(CHUNKS):
                        tail.normalise(dve, c.shift(-1))
                    dve.wait_ge(inverted, done(c))
                    if c.shift(-1).exists:
                        dve.wait_ge(xs_T, done(c.shift(-1)))
                    for k in range(PER):
                        last = dve.tensor_scalar(xs[:, k, :], inp.x[:, p, k, :], inv[:, k:k + 1], math.sqrt(D),
                                                 ALU.mult, ALU.mult)
                    last.then_inc(n_steps, 1)
                    dve.wait_ge(n_steps, steps.next())
                    hold(dve)
                    steps = StepCount(c, 3)
                    dve.wait_ge(gated, done(c))
                    dve.memset(gate[:, :].rearrange("p (b s) -> p b s", s=S)[:, :, 0:1], 0.0).then_inc(s_steps, 1)
                    dve.wait_ge(s_steps, steps.next())
                    hold(dve)
                    dve.tensor_tensor_scan(h[:, :], gate[:, :], kv_bank[:, :], 0.0, ALU.mult, ALU.add)\
                        .then_inc(s_steps, 1)
                    dve.wait_ge(s_steps, steps.next())
                    hold(dve)
                    if c.shift(-1).exists:
                        dve.wait_ge(y_ready, done(c.shift(-1)))
                    dve.tensor_tensor(out[:, :], q_bank[:, :], h[:, :], ALU.mult).then_inc(s_steps, 1)
                    dve.wait_ge(s_steps, steps.next())
                    hold(dve)
                    dve.wait_ge(y_ready, done(c))
                    if c.shift(-2).exists:
                        dve.wait_ge(tail.normed, done(c.shift(-2)))
                    dve.tensor_tensor(tail.r[:, p, :, :], per_tile(y_bank[:, :]), x, ALU.add).then_inc(tail.summed, 1)
                    tail.moments(dve, c)

                chunk_loop(dve, body)
                tail.normalise(dve, last_chunk())

            @block.gpsimd
            def _(pool):
                def body(c):
                    pool.wait_ge(n_steps, nth(c, 4, 3))
                    hold(pool)
                    if c.shift(-1).exists:
                        pool.wait_ge(n_steps, nth(c.shift(-1), 4, 4))
                        hold(pool)
                    pool.tensor_tensor(inv[:, :], ss_max[:, :], net.minus_half[:, 0:PER], ALU.pow).then_inc(inverted, 1)
                    tail.inverse_std(pool, c)

                chunk_loop(pool, body)


def conv_moe(net, final, name):
    nc, dram = net.nc, net.dram
    E, K, HID = EXPERTS, 3, 32

    def op(what):
        return dram[f"{name}_{what}"]

    def column(v):
        return v.rearrange("(p o) -> p o", o=1)

    with ExitStack() as ctx:
        sub = Sublayer(net, ctx, name)
        sb, sem, bank = sub.sb, sub.sem, sub.bank
        taps = sub.load("taps", [128, K], op("dw_kernel").rearrange("d o k -> d (o k)"))
        dw_b = sub.load("dw_b", [128, 1], column(op("dw_bias")))
        pw_s = sub.load("pw_w", [128, D], op("pw_wT"))
        pw_b = sub.load("pw_b", [128, 1], column(op("pw_b")))
        router_s = sub.load("router_w", [128, E], op("router_wT"))
        router_b = sub.row("router_b", op("router_b"), E)
        experts_s = sub.load("expert_w", [128, E, D], op("expert_wT"))
        expert_b = sub.load("expert_b", [3, E * D], op("expert_b").rearrange("(o e) d -> o (e d)", o=1)
                            .to_broadcast([3, E * D]))
        high, middle = sb("expert_b_high", [3, E * D], BF16), sb("expert_b_middle", [3, E * D], BF16)
        rest, low = sb("expert_b_rest", [3, E * D]), sb("expert_b_low", [3, E * D])
        parts_b, ones_b = sb("expert_b_parts", [3, E * D], BF16), sb("ones_bf", [3, 128], BF16)
        split_steps = sem("bias_split_steps")
        out_s = sub.load("out_w", [128, D], op("out_wT"))
        out_b = sub.load("out_b", [1, D], op("out_b").rearrange("(o d) -> o d", o=1))
        norm_w = sub.row("norm_w", op("norm_w"), D)
        down_s = sub.load("down_w", [128, HID], op("ff_down_wT"))
        down_b = sub.load("down_b", [HID, 1], column(op("ff_down_b")))
        up_s = sub.load("up_w", [HID, D], op("ff_up_wT"))
        up_b = sub.row("up_b", op("ff_up_b"), D)
        router = Router(sub, E)
        conv, pointwise = sb("conv", [128, CHUNK]), sb("pointwise", [128, CHUNK])
        x1_T = sb("x1_T", [128, 2, CHUNK])
        mix = sb("mix", [128, PER, E])
        expert_out = sb("expert_out", [128, 2, PER, E, D])
        combined, combined_T = sb("combined", [128, PER, D]), sb("combined_T", [128, CHUNK])
        z_sq, ms = sb("z_sq", [128, PER, D]), sb("ms", [128, PER])
        ms_eps, rms_inv = sb("ms_eps", [128, PER]), sb("rms_inv", [128, PER])
        h, h_T = sb("h", [128, PER, D]), sb("h_T", [128, CHUNK])
        down = sb("down", [HID, CHUNK])
        x_res, hx = sb("x_res", [128, 2, PER, D]), sb("h_plus_x", [128, PER, D])
        inp, tail = ChunkInput(sub), ChunkTail(sub, final)

        pw_bank, route_bank = bank("pw"), bank("route")
        expert_bank = [bank("experts0"), bank("experts1")]
        turn_bank = bank("turned")
        z_bank = bank("z")
        ff_bank = bank("ff")
        xT_bank = bank("xT")
        conv_steps, r_steps, comb_steps = sem("conv_steps"), router.steps, sem("combine_steps")
        pw_ready, pw_done, routed, exp_done = sem("pw_ready"), sem("pw_done"), sem("logits_ready"), sem("exp_done")
        expert_ready, expert_done = sem("experts_ready"), sem("experts_done")
        combT_ready, combT_copied, z_ready, squared = sem("combT_ready"), sem("combT_copied"), sem("z_ready"), sem("squared")
        ms_done, ms_eps_done, rms_done, h_done = sem("ms_done"), sem("ms_eps_done"), sem("rms_done"), sem("h_done")
        hT_ready, hT_copied, down_ready, down_done = sem("hT_ready"), sem("hT_copied"), sem("down_ready"), sem("down_done")
        up_ready, biased, hx_done = sem("up_ready"), sem("biased"), sem("h_plus_x_done")
        R = Router.RANKED + Router.TWO
        with nc.Block() as block:
            stream(sub, block, inp, tail, [(biased, 1), (conv_steps, 4)], early=True)

            @block.tensor
            def _(pe):
                sub.await_weights(pe)

                def pointwise_product(c):
                    pe.wait_ge(conv_steps, nth(c, 4, 3))
                    if c.shift(-1).exists:
                        pe.wait_ge(pw_done, done(c.shift(-1)))
                    pe.matmul(pw_bank[:, :], pw_s[:, :], conv[:, :], start=True, stop=True).then_inc(pw_ready, 1)

                def logits(c):
                    pe.wait_ge(conv_steps, nth(c, 4, 4))
                    if c.shift(-1).exists:
                        pe.wait_ge(r_steps, nth(c.shift(-1), R, 1))
                    for k in range(PER):
                        last = pe.matmul(route_bank[:, E * k:E * k + E], x1_T[:, c.u % 2, TILE * k:TILE * k + TILE],
                                         router_s[:, :], start=True, stop=True)
                    last.then_inc(routed, 1)

                def experts(c, k):
                    for g in range(2):
                        n = 2 * k + g
                        if n >= 2:
                            pe.wait_ge(expert_done, nth(c, 2 * PER, n - 1))
                        elif c.shift(-1).exists:
                            pe.wait_ge(expert_done, nth(c.shift(-1), 2 * PER, 2 * PER + n - 1))
                        pe.matmul(expert_bank[g][:, :], x1_T[:, c.u % 2, TILE * k:TILE * k + TILE],
                                  experts_s[:, 4 * g:4 * g + 4, :].rearrange("p e d -> p (e d)"),
                                  start=True, stop=False)
                        pe.matmul(expert_bank[g][:, :], ones_b[:, :], parts_b[:, 512 * g:512 * g + 512],
                                  start=False, stop=True).then_inc(expert_ready, 1)

                def body(c):
                    x1 = [x1_T[:, c.u % 2, TILE * k:TILE * k + TILE] for k in range(PER)]
                    ahead = c.shift(1).inside(CHUNKS)
                    if ahead:
                        logits(c.shift(1))
                        experts(c.shift(1), 0)
                        experts(c.shift(1), 1)
                    pe.wait_ge(comb_steps, nth(c, E, E))
                    if c.shift(-1).exists:
                        pe.wait_ge(hT_copied, done(c.shift(-1)))
                    for k in range(PER):
                        last = pe.transpose(turn_bank[:, TILE * k:TILE * k + TILE], combined[:, k, :], net.ident[:, :])
                    last.then_inc(combT_ready, 1)
                    if ahead:
                        experts(c.shift(1), 2)
                    pe.wait_ge(combT_copied, done(c))
                    if c.shift(-1).exists:
                        pe.wait_ge(h_done, done(c.shift(-1)))
                    for k in range(PER):
                        z = z_bank[:, D * k:D * k + D]
                        pe.matmul(z, x1[k], net.ident[:, :], start=True, stop=False)
                        pe.matmul(z, combined_T[:, TILE * k:TILE * k + TILE], out_s[:, :], start=False, stop=False)
                        last = pe.matmul(z, net.ones[0:1, :], out_b[:, :], start=False, stop=True)
                    last.then_inc(z_ready, 1)
                    if ahead:
                        experts(c.shift(1), 3)
                    if c.shift(-1).inside(CHUNKS):
                        tail.transpose(pe, c.shift(-1), xT_bank)
                    pe.wait_ge(h_done, done(c))
                    for k in range(PER):
                        last = pe.transpose(turn_bank[:, TILE * k:TILE * k + TILE], h[:, k, :], net.ident[:, :])
                    last.then_inc(hT_ready, 1)
                    if c.shift(2).inside(CHUNKS):
                        pointwise_product(c.shift(2))
                    pe.wait_ge(hT_copied, done(c))
                    if c.shift(-1).exists:
                        pe.wait_ge(tail.summed, done(c.shift(-1)))
                    pe.matmul(ff_bank[0:HID, :], down_s[:, :], h_T[:, :], start=True, stop=True).then_inc(down_ready, 1)
                    pe.wait_ge(down_done, done(c))
                    for k in range(PER):
                        last = pe.matmul(ff_bank[:, D * k:D * k + D], down[:, TILE * k:TILE * k + TILE], up_s[:, :],
                                         start=True, stop=True)
                    last.then_inc(up_ready, 1)

                first, second = first_chunks()
                pointwise_product(first)
                pointwise_product(second)
                logits(first)
                pe.wait_ge(split_steps, 8)
                for k in range(PER):
                    experts(first, k)
                chunk_loop(pe, body)
                tail.transpose(pe, last_chunk(), xT_bank)

            @block.scalar
            def _(act):
                sub.await_weights(act)

                def pointwise_silu(c):
                    act.wait_ge(pw_ready, done(c))
                    if c.shift(-1).exists:
                        act.wait_ge(conv_steps, nth(c.shift(-1), 4, 4))
                    act.activation(pointwise[:, :], pw_bank[:, :], ACT.Silu, bias=pw_b[:, 0:1]).then_inc(pw_done, 1)

                def experts_silu(c, k):
                    if k == 0 and c.shift(-2).exists:
                        act.wait_ge(comb_steps, nth(c.shift(-2), E, E))
                    for g in range(2):
                        act.wait_ge(expert_ready, nth(c, 2 * PER, 2 * k + g + 1))
                        act.activation(expert_out[:, c.u % 2, k, 4 * g:4 * g + 4, :].rearrange("p e d -> p (e d)"),
                                       expert_bank[g][:, :], ACT.Silu).then_inc(expert_done, 1)

                def exponentials(c):
                    act.wait_ge(r_steps, nth(c, R, Router.RANKED))
                    act.activation(router.exps[:, :, :], router.shifted[:, :, :], ACT.Exp).then_inc(exp_done, 1)

                def body(c):
                    ahead = c.shift(1).inside(CHUNKS)
                    if ahead:
                        experts_silu(c.shift(1), 0)
                        experts_silu(c.shift(1), 1)
                    act.wait_ge(combT_ready, done(c))
                    if c.shift(-1).exists:
                        act.wait_ge(z_ready, done(c.shift(-1)))
                    act.activation(combined_T[:, :], turn_bank[:, :], ACT.Copy).then_inc(combT_copied, 1)
                    if ahead:
                        experts_silu(c.shift(1), 2)
                    act.wait_ge(z_ready, done(c))
                    act.activation(z_sq[:, :, :].rearrange("p k d -> p (k d)"), z_bank[:, :], ACT.Square)\
                        .then_inc(squared, 1)
                    if ahead:
                        experts_silu(c.shift(1), 3)
                    if c.shift(-1).inside(CHUNKS):
                        tail.copy_transposed(act, c.shift(-1), xT_bank)
                    act.wait_ge(hT_ready, done(c))
                    act.activation(h_T[:, :], turn_bank[:, :], ACT.Copy).then_inc(hT_copied, 1)
                    if c.shift(2).inside(CHUNKS):
                        pointwise_silu(c.shift(2))
                    if ahead:
                        exponentials(c.shift(1))
                    act.wait_ge(down_ready, done(c))
                    act.activation(down[:, :], ff_bank[0:HID, :], ACT.Gelu, bias=down_b[:, 0:1]).then_inc(down_done, 1)

                first, second = first_chunks()
                pointwise_silu(first)
                pointwise_silu(second)
                for k in range(PER):
                    experts_silu(first, k)
                exponentials(first)
                chunk_loop(act, body)
                tail.copy_transposed(act, last_chunk(), xT_bank)

            @block.vector
            def _(dve):
                sub.await_weights(dve)

                def convolve(c):
                    x = inp.xT[:, c.u % 2, :]
                    seqs = x.rearrange("p (b s) -> p b s", s=S)
                    sums = conv[:, :].rearrange("p (b s) -> p b s", s=S)
                    dve.wait_ge(inp.loaded[c.u % 2], landed(c, inp.dmas))
                    steps = StepCount(c, 4)
                    if c.shift(-1).exists:
                        dve.wait_ge(pw_ready, done(c.shift(-1)))
                    dve.tensor_scalar(conv[:, :], x, taps[:, 2:3], dw_b[:, 0:1], ALU.mult, ALU.add)\
                        .then_inc(conv_steps, 1)
                    dve.wait_ge(conv_steps, steps.next())
                    hold(dve)
                    for back in (1, 2):
                        dve.scalar_tensor_tensor(sums[:, :, back:S], seqs[:, :, 0:S - back],
                                                 taps[:, 2 - back:3 - back], sums[:, :, back:S],
                                                 ALU.mult, ALU.add).then_inc(conv_steps, 1)
                        dve.wait_ge(conv_steps, steps.next())
                        hold(dve)
                    return steps

                def add_pointwise(c, steps):
                    p = c.u % 2
                    dve.wait_ge(pw_done, done(c))
                    if c.shift(-2).exists:
                        dve.wait_ge(z_ready, done(c.shift(-2)))
                    dve.tensor_tensor(x1_T[:, p, :], pointwise[:, :], inp.xT[:, p, :], ALU.add).then_inc(conv_steps, 1)
                    dve.wait_ge(conv_steps, steps.next())
                    hold(dve)

                def rank(c, steps):
                    dve.wait_ge(routed, done(c))
                    router.rank(dve, steps, route_bank[:, 0:PER * E].rearrange("p (k e) -> p k e", k=PER), router_b[:, :])

                def mix_experts(c, steps):
                    router.mix_two(dve, steps, mix[:, :, :], lambda: dve.wait_ge(exp_done, done(c)))

                def body(c):
                    p = c.u % 2
                    if c.shift(-1).inside(CHUNKS):
                        tail.normalise(dve, c.shift(-1))
                    combine = StepCount(c, E)
                    dve.wait_ge(expert_done, nth(c, 2 * PER, 2 * PER))
                    if c.shift(-1).exists:
                        dve.wait_ge(combT_ready, done(c.shift(-1)))
                    for e in range(E):
                        for k in range(PER):
                            if e == 0:
                                last = dve.tensor_scalar(combined[:, k, :], expert_out[:, p, k, e, :], mix[:, k, e:e + 1],
                                                         None, ALU.mult)
                            else:
                                last = dve.scalar_tensor_tensor(combined[:, k, :], expert_out[:, p, k, e, :],
                                                                mix[:, k, e:e + 1], combined[:, k, :],
                                                                ALU.mult, ALU.add)
                        last.then_inc(comb_steps, 1)
                        dve.wait_ge(comb_steps, combine.next())
                        hold(dve)
                    dve.wait_ge(squared, done(c))
                    if c.shift(-1).exists:
                        dve.wait_ge(ms_eps_done, done(c.shift(-1)))
                    dve.tensor_reduce(ms[:, :], z_sq[:, :, :], AX_X, ALU.add).then_inc(ms_done, 1)
                    if c.shift(2).inside(CHUNKS):
                        convolved = convolve(c.shift(2))
                    dve.wait_ge(rms_done, done(c))
                    if c.shift(-1).exists:
                        dve.wait_ge(hx_done, done(c.shift(-1)))
                    for k in range(PER):
                        last = dve.scalar_tensor_tensor(h[:, k, :], z_bank[:, D * k:D * k + D], rms_inv[:, k:k + 1],
                                                        norm_w[:, :], ALU.mult, ALU.mult)
                    last.then_inc(h_done, 1)
                    steps = StepCount(c.shift(1), R)
                    if c.shift(1).inside(CHUNKS):
                        rank(c.shift(1), steps)
                    if c.shift(2).inside(CHUNKS):
                        add_pointwise(c.shift(2), convolved)
                    if c.shift(1).inside(CHUNKS):
                        mix_experts(c.shift(1), steps)
                    dve.wait_ge(hx_done, done(c))
                    dve.wait_ge(up_ready, done(c))
                    if c.shift(-2).exists:
                        dve.wait_ge(tail.normed, done(c.shift(-2)))
                    dve.tensor_tensor(tail.r[:, p, :, :], per_tile(ff_bank[:, :]), hx[:, :, :], ALU.add)\
                        .then_inc(tail.summed, 1)
                    tail.moments(dve, c)

                first, second = first_chunks()
                ahead = convolve(first)
                dve.tensor_copy(high[:, :], expert_b[:, :]).then_inc(split_steps, 1)
                dve.wait_ge(split_steps, 1)
                dve.tensor_tensor(rest[:, :], expert_b[:, :], high[:, :], ALU.subtract).then_inc(split_steps, 1)
                dve.wait_ge(split_steps, 2)
                dve.tensor_copy(middle[:, :], rest[:, :]).then_inc(split_steps, 1)
                dve.wait_ge(split_steps, 3)
                dve.tensor_tensor(low[:, :], rest[:, :], middle[:, :], ALU.subtract).then_inc(split_steps, 1)
                dve.wait_ge(split_steps, 4)
                dve.tensor_scalar(parts_b[:, :], high[:, :], net.ident[0:3, 0:1], None, ALU.mult)\
                    .then_inc(split_steps, 1)
                dve.wait_ge(split_steps, 5)
                dve.scalar_tensor_tensor(parts_b[:, :], middle[:, :], net.ident[0:3, 1:2], parts_b[:, :],
                                         ALU.mult, ALU.add).then_inc(split_steps, 1)
                dve.wait_ge(split_steps, 6)
                dve.scalar_tensor_tensor(parts_b[:, :], low[:, :], net.ident[0:3, 2:3], parts_b[:, :],
                                         ALU.mult, ALU.add).then_inc(split_steps, 1)
                dve.memset(ones_b[:, :], 1.0).then_inc(split_steps, 1)
                add_pointwise(first, ahead)
                add_pointwise(second, convolve(second))
                steps = StepCount(first, R)
                rank(first, steps)
                mix_experts(first, steps)
                chunk_loop(dve, body)
                tail.normalise(dve, last_chunk())

            @block.gpsimd
            def _(pool):
                sub.await_weights(pool)

                def body(c):
                    p = c.u % 2
                    pool.wait_ge(inp.loaded[c.u % 2], landed(c, inp.dmas))
                    hold(pool)
                    if c.shift(-2).exists:
                        pool.wait_ge(hx_done, done(c.shift(-2)))
                        hold(pool)
                    pool.tensor_tensor(x_res[:, p, :, :], inp.x[:, p, :, :], up_b[:, :].rearrange("p (o d) -> p o d", o=1)
                                       .to_broadcast([128, PER, D]), ALU.add).then_inc(biased, 1)
                    pool.wait_ge(ms_done, done(c))
                    hold(pool)
                    pool.tensor_scalar(ms_eps[:, :], ms[:, :], 1.0 / D, 1e-6, ALU.mult, ALU.add).then_inc(ms_eps_done, 1)
                    pool.wait_ge(ms_eps_done, done(c))
                    hold(pool)
                    if c.shift(-1).exists:
                        pool.wait_ge(h_done, done(c.shift(-1)))
                        hold(pool)
                    pool.tensor_tensor(rms_inv[:, :], ms_eps[:, :], net.minus_half[:, 0:PER], ALU.pow).then_inc(rms_done, 1)
                    pool.wait_ge(h_done, done(c))
                    hold(pool)
                    pool.wait_ge(biased, done(c))
                    hold(pool)
                    if c.shift(-1).exists:
                        pool.wait_ge(tail.summed, done(c.shift(-1)))
                        hold(pool)
                    pool.tensor_tensor(hx[:, :, :], h[:, :, :], x_res[:, p, :, :], ALU.add).then_inc(hx_done, 1)
                    tail.inverse_std(pool, c)

                chunk_loop(pool, body)


def single_head(net, final, name):
    nc, dram = net.nc, net.dram
    scale = 1.0 / math.sqrt(D)

    def op(what):
        return dram[f"{name}_{what}"]

    with ExitStack() as ctx:
        sub = Sublayer(net, ctx, name)
        sb, sem, bank = sub.sb, sub.sem, sub.bank
        w_s = [sub.load(k, [128, D], op(k)) for k in ("Wq", "Wk", "Wv")]
        b_s = [sub.load(k, [128, 1], op(k).rearrange("(p o) -> p o", o=1)) for k in ("bq", "bk")]
        bv = sub.row("bv", op("bv"), D)
        qk = [sb("q_T", [128, CHUNK]), sb("k_T", [128, CHUNK])]
        v = sb("v", [128, 2, PER, D])
        maxima, shifted = sb("maxima", [128, PER]), sb("shifted", [128, PER, S])
        probs = sb("probs", [128, 2, PER, TILE])
        sums, recip = sb("sums", [128, PER]), sb("recip", [128, PER])
        probs_T = sb("probs_T", [128, PER, TILE])
        x_res = sb("x_res", [128, 2, PER, D])
        inp, tail = ChunkInput(sub, cross=True), ChunkTail(sub, final)
        qk_bank, v_bank, score_bank = [bank("q_ps"), bank("k_ps")], bank("v_ps"), bank("scores")
        pT_bank, o_bank, xT_bank = bank("pT"), bank("o_ps"), bank("xT")
        cleared, projected, copied = sem("cleared"), sem("projected"), sem("projections_copied")
        scored, shift_steps, exped = sem("scores_ready"), sem("shift_steps"), sem("probs_ready")
        turned, turned_copied, mixed = sem("probs_transposed"), sem("probs_T_copied"), sem("values_mixed")
        sum_steps, biased = sem("sum_steps"), sem("biased")
        with nc.Block() as block:
            stream(sub, block, inp, tail, [(biased, 1), (projected, 1)])

            @block.tensor
            def _(pe):
                sub.await_weights(pe)

                def scores(c):
                    p = c.u % 2
                    pe.wait_ge(inp.loaded[c.u % 2], landed(c, inp.dmas))
                    if c.shift(-1).exists:
                        pe.wait_ge(copied, done(c.shift(-1), 3))
                    for r, src in ((0, inp.xT), (1, inp.cT)):
                        pe.matmul(qk_bank[r][:, :], w_s[r][:, :], src[:, p, :], start=True, stop=True)
                    for k in range(PER):
                        last = pe.matmul(v_bank[:, D * k:D * k + D], inp.cT[:, p, TILE * k:TILE * k + TILE], w_s[2][:, :],
                                         start=True, stop=True)
                    last.then_inc(projected, 1)
                    pe.wait_ge(copied, done(c, 3))
                    if c.shift(-1).exists:
                        pe.wait_ge(shift_steps, nth(c.shift(-1), 2, 2))
                    for k in range(PER):
                        for b in range(2):
                            seq = slice(TILE * k + S * b, TILE * k + S * b + S)
                            last = pe.matmul(score_bank[S * b:S * b + S, S * k:S * k + S], qk[0][:, seq], qk[1][:, seq],
                                             start=True, stop=True)
                    last.then_inc(scored, 1)

                def body(c):
                    p = c.u % 2
                    if c.shift(1).inside(CHUNKS):
                        scores(c.shift(1))
                    pe.wait_ge(exped, done(c, 2))
                    if c.shift(-1).exists:
                        pe.wait_ge(turned_copied, done(c.shift(-1)))
                    for k in range(PER):
                        last = pe.transpose(pT_bank[:, TILE * k:TILE * k + TILE], probs[:, p, k, :], net.ident[:, :])
                    last.then_inc(turned, 1)
                    if c.shift(-1).inside(CHUNKS):
                        tail.transpose(pe, c.shift(-1), xT_bank)
                    pe.wait_ge(turned_copied, done(c))
                    if c.shift(-1).exists:
                        pe.wait_ge(tail.summed, done(c.shift(-1)))
                    for k in range(PER):
                        last = pe.matmul(o_bank[:, D * k:D * k + D], probs_T[:, k, :], v[:, p, k, :],
                                         start=True, stop=True)
                    last.then_inc(mixed, 1)

                scores(first_chunks()[0])
                chunk_loop(pe, body)
                tail.transpose(pe, last_chunk(), xT_bank)

            @block.scalar
            def _(act):
                sub.await_weights(act)
                act.wait_ge(cleared, 1)

                def copy_projected(c):
                    act.wait_ge(projected, done(c))
                    if c.shift(-1).exists:
                        act.wait_ge(scored, done(c.shift(-1)))
                    for r in range(2):
                        act.activation(qk[r][:, :], qk_bank[r][:, :], ACT.Identity, bias=b_s[r][:, 0:1]).then_inc(copied, 1)
                    if c.shift(-2).exists:
                        act.wait_ge(mixed, done(c.shift(-2)))
                    act.activation(v[:, c.u % 2, :, :].rearrange("p k d -> p (k d)"), v_bank[:, :], ACT.Copy)\
                        .then_inc(copied, 1)

                def exponentials(c):
                    act.wait_ge(shift_steps, nth(c, 2, 2))
                    if c.shift(-2).exists:
                        act.wait_ge(turned, done(c.shift(-2)))
                    if c.shift(-2).exists:
                        act.wait_ge(sum_steps, nth(c.shift(-2), 2, 1))
                    for b in range(2):
                        half = slice(S * b, S * b + S)
                        act.activation(probs[half, c.u % 2, :, half], shifted[half, :, :], ACT.Exp, scale=scale)\
                            .then_inc(exped, 1)

                def body(c):
                    if c.shift(1).inside(CHUNKS):
                        copy_projected(c.shift(1))
                    act.wait_ge(turned, done(c))
                    if c.shift(-1).exists:
                        act.wait_ge(mixed, done(c.shift(-1)))
                    act.activation(probs_T[:, :, :].rearrange("p k t -> p (k t)"), pT_bank[:, :], ACT.Copy)\
                        .then_inc(turned_copied, 1)
                    if c.shift(1).inside(CHUNKS):
                        exponentials(c.shift(1))
                    if c.shift(-1).inside(CHUNKS):
                        tail.copy_transposed(act, c.shift(-1), xT_bank)

                copy_projected(first_chunks()[0])
                exponentials(first_chunks()[0])
                chunk_loop(act, body)
                tail.copy_transposed(act, last_chunk(), xT_bank)

            @block.vector
            def _(dve):
                sub.await_weights(dve)

                def shift(c):
                    dve.wait_ge(scored, done(c))
                    if c.shift(-1).exists:
                        dve.wait_ge(exped, done(c.shift(-1), 2))
                    steps = StepCount(c, 2)
                    got = score_bank[:, 0:PER * S].rearrange("p (k s) -> p k s", k=PER)
                    dve.tensor_reduce(maxima[:, :], got, AX_X, ALU.max).then_inc(shift_steps, 1)
                    dve.wait_ge(shift_steps, steps.next())
                    hold(dve)
                    dve.tensor_tensor(shifted[:, :, :], got, spread_last(maxima[:, :], S), ALU.subtract)\
                        .then_inc(shift_steps, 1)
                    dve.wait_ge(shift_steps, steps.next())
                    hold(dve)

                def body(c):
                    p = c.u % 2
                    if c.shift(-1).inside(CHUNKS):
                        tail.normalise(dve, c.shift(-1))
                    if c.shift(1).inside(CHUNKS):
                        shift(c.shift(1))
                    steps = StepCount(c, 2)
                    dve.wait_ge(exped, done(c, 2))
                    dve.tensor_reduce(sums[:, :], probs[:, p, :, :], AX_X, ALU.add).then_inc(sum_steps, 1)
                    dve.wait_ge(sum_steps, steps.next())
                    hold(dve)
                    dve.reciprocal(recip[:, :], sums[:, :]).then_inc(sum_steps, 1)
                    dve.wait_ge(sum_steps, steps.next())
                    hold(dve)
                    dve.wait_ge(mixed, done(c))
                    dve.wait_ge(biased, done(c))
                    if c.shift(-2).exists:
                        dve.wait_ge(tail.normed, done(c.shift(-2)))
                    for k in range(PER):
                        last = dve.scalar_tensor_tensor(tail.r[:, p, k, :], o_bank[:, D * k:D * k + D], recip[:, k:k + 1],
                                                        x_res[:, p, k, :], ALU.mult, ALU.add)
                    last.then_inc(tail.summed, 1)
                    tail.moments(dve, c)

                shift(first_chunks()[0])
                chunk_loop(dve, body)
                tail.normalise(dve, last_chunk())

            @block.gpsimd
            def _(pool):
                pool.memset(probs[:, :, :, :], 0.0).then_inc(cleared, 1)
                sub.await_weights(pool)

                def body(c):
                    p = c.u % 2
                    pool.wait_ge(inp.loaded[c.u % 2], landed(c, inp.dmas))
                    hold(pool)
                    if c.shift(-2).exists:
                        pool.wait_ge(tail.summed, done(c.shift(-2)))
                        hold(pool)
                    pool.tensor_tensor(x_res[:, p, :, :], inp.x[:, p, :, :], bv[:, :].rearrange("p (o d) -> p o d", o=1)
                                       .to_broadcast([128, PER, D]), ALU.add).then_inc(biased, 1)
                    tail.inverse_std(pool, c)

                chunk_loop(pool, body)



def constants():
    c = {}
    c["c_ident"] = np.eye(128, dtype=np.float32)
    p = np.arange(128)
    c["c_headmask"] = ((p[:, None] // 8) % 8 == np.arange(8)[None, :]).astype(np.float32)
    i, j = np.arange(S)[:, None], np.arange(S)[None, :]
    keep = (j < i) | ((i == 0) & (j == 0))
    c["c_causal"] = np.tile(np.where(keep, BIG, -1e30).astype(np.float32), (2, 1))
    slopes = np.exp2(-(np.arange(1, HEADS + 1, dtype=np.float32)))
    alibi = -np.abs(i - j).astype(np.float32)[:, None, :] * slopes[None, :, None]
    c["c_alibi"] = np.tile(alibi.reshape(S, HEADS * S).astype(np.float32), (2, 1))
    inv_freq = (1.0 / np.float32(10000.0) ** (np.arange(0, HD, 2, dtype=np.float32) / HD)).astype(np.float32)
    pos = np.arange(S, dtype=np.float32)
    freqs = np.repeat(pos[:, None] * inv_freq[None, :], 2, axis=-1)
    sv = ((np.arange(0, HD, 2, dtype=np.float32) + np.float32(0.4 * HD)) / np.float32(1.4 * HD)).astype(np.float32)
    power = ((pos - S // 2) / np.float32(512.0)).astype(np.float32)
    length = (sv[None, :] ** power[:, None]).astype(np.float32)
    length = np.concatenate([length, length], axis=-1)
    cos, sin = np.cos(freqs).astype(np.float32), np.sin(freqs).astype(np.float32)
    sign = np.where(np.arange(HD) % 2 == 0, -1.0, 1.0).astype(np.float32)[None, :]
    root = np.float32(HD ** -0.5)
    parts = [cos * length * root, cos / length, sin * sign * length * root, sin * sign / length]
    c["c_rope"] = np.concatenate([np.tile(t.T, (HEADS, 1)) for t in parts], axis=1).astype(np.float32)
    c["c_esel"] = np.repeat(np.eye(32, dtype=np.float32), 32, axis=1)
    c["c_before"] = (p[:, None] <= p[None, :]).astype(np.float32)
    c["c_iota"] = np.tile(np.arange(32, dtype=np.float32)[None, :], (128, 1))
    return {k: np.ascontiguousarray(v, dtype=np.float32) for k, v in c.items()}


def build_program(nc, dram):
    with ExitStack() as ctx:
        net = Net(nc, ctx, dram)
        loaded, set_up = nc.alloc_semaphore("stream_loaded"), nc.alloc_semaphore("set_up")
        for eng in (nc.tensor, nc.vector, nc.gpsimd, nc.sync):
            SCRATCH[eng.engine] = eng.alloc_register(f"scratch_{eng.engine.name}")
            eng.reg_mov(SCRATCH[eng.engine], 1)
        with nc.Block() as block:
            @block.sync
            def _(sp):
                sp.dma_start(net.x_tok[:, :, :], dram["x"].rearrange("(t p) d -> p t d", p=128)).then_inc(loaded, 16)
                sp.dma_start(net.x_T[:, :], dram["x_T"]).then_inc(loaded, 16)
                sp.dma_start(net.ident[:, :], dram["c_ident"]).then_inc(loaded, 16)
                sp.dma_start(net.headmask[:, :], dram["c_headmask"]).then_inc(loaded, 16)
                sp.wait_ge(loaded, 64)

            @block.gpsimd
            def _(pool):
                pool.memset(net.ones[:, :], 1.0).then_inc(set_up, 1)
                pool.memset(net.minus_half[:, :], -0.5).then_inc(set_up, 1)
                pool.wait_ge(set_up, 2)

        w = dram
        root = HD ** -0.5

        def halves(m, dv=HD):
            v = m.rearrange("i (k r d) -> i k r d", r=2, d=dv)
            return [v[:, :, r, :] for r in range(2)]

        def run(n, final):
            if n == 1:
                moe(net, final, "L0_attn", w["L0_attn_gate_w"], w["L0_attn_w1"], w["L0_attn_b1"], w["L0_attn_w2"],
                    w["L0_attn_b2"], ACT.Gelu_apprx_tanh, gate_b=w["L0_attn_gate_b"], top=2)
            if n == 2:
                single_head(net, final, "L0_xattn")
            if n == 3:
                ternary_ffn(net, final, "L0_ffn")
            if n == 4:
                v = w["L1_attn_WvT"]
                attention(net, final, "L1_attn", w["L1_attn_WqT"], w["L1_attn_WkT"], [v, v], dv=2 * HD,
                          wo=w["L1_attn_WoT"], rope=True,
                          lambdas=[w["L1_attn_lambda_q1"], w["L1_attn_lambda_k1"], w["L1_attn_lambda_q2"],
                                   w["L1_attn_lambda_k2"]])
            if n == 5:
                attention(net, final, "L1_xattn", w["L1_xattn_W_q"], w["L1_xattn_W_k"], halves(w["L1_xattn_W_v"]),
                          bv=w["L1_xattn_b_v"], wo=w["L1_xattn_W_o"], bo=w["L1_xattn_b_o"], cross=True, scale=root,
                          mask=("min", "causal"))
            if n == 6:
                moe_small(net, final, "L1_ffn")
            if n == 7:
                k = w["L2_attn_WkT"].rearrange("i (k d) -> i k d", k=8)
                v = w["L2_attn_WvT"]
                attention(net, final, "L2_attn", w["L2_attn_WqT"], [k, k], [v, v], wo=w["L2_attn_WoT"],
                          bo=w["L2_attn_bo"], scale=root, mask=("add", "c_alibi"))
            if n == 8:
                attention(net, final, "L2_xattn", w["L2_xattn_q_wT"], w["L2_xattn_k_wT"], halves(w["L2_xattn_v_wT"]),
                          bq=w["L2_xattn_q_b"], bk=w["L2_xattn_k_b"], bv=w["L2_xattn_v_b"], cross=True, scale=root,
                          mask=("min", "keys"))
            if n == 9:
                conv_moe(net, final, "L2_ffn")
            if n == 10:
                gated_scan(net, final, "L3_attn")
            if n == 11:
                attention(net, final, "L3_xattn", w["L3_xattn_Wq"], w["L3_xattn_Wk"], halves(w["L3_xattn_Wv"]),
                          bq=w["L3_xattn_bq"], bk=w["L3_xattn_bk"], bv=w["L3_xattn_bv"], wo=w["L3_xattn_Wo"],
                          bo=w["L3_xattn_bo"], cross=True, scale=root, mask=("min", "full"))
            if n == 12:
                moe(net, final, "L3_ffn", w["L3_ffn_wg"], w["L3_ffn_W1"], w["L3_ffn_b1"], w["L3_ffn_W2"], w["L3_ffn_b2"],
                    ACT.Gelu, top=1)

        for n in N_SUBLAYERS:
            run(n, n == N_SUBLAYERS[-1])
            net.end_sublayer()
        for eng in (nc.tensor, nc.vector, nc.gpsimd, nc.sync):
            eng.wait_ge(set_up, SCRATCH[eng.engine])


_TRANSPOSED = ["L1_attn_Wq", "L1_attn_Wk", "L1_attn_Wv", "L1_attn_Wo", "L2_attn_Wq", "L2_attn_Wk", "L2_attn_Wv",
               "L2_attn_Wo", "L2_xattn_q_w", "L2_xattn_k_w", "L2_xattn_v_w", "L0_ffn_W1", "L0_ffn_W2",
               "L1_ffn_router_w", "L2_ffn_pw_w", "L2_ffn_router_w", "L2_ffn_out_w", "L2_ffn_ff_down_w",
               "L2_ffn_ff_up_w", "L3_attn_W_qkva"]


def kernel(**inputs):
    import concourse.bacc as _bacc
    from concourse.bass_utils import run_bass_kernel_spmd as _run

    nc = _bacc.Bacc("TRN2", target_bir_lowering=False, num_devices=1)
    arrays = {}
    for name, value in inputs.items():
        a = np.asarray(value)
        if name == "x":
            a = a.reshape(TOKENS, D)
            arrays["x_T"] = a.T
        elif name == "ctx_1024":
            name, a = "ctx_T", a.reshape(TOKENS, D).T
        elif name == "mask_BxS2_ik0":
            name = "mask_keys"
        elif name == "mask_Bx1xSxS2_bk0":
            name, a = "mask_full", a.reshape(TOKENS, S)
        elif name in _TRANSPOSED:
            name, a = name + "T", a.T
        elif name == "L2_ffn_expert_w":
            name, a = name + "T", a.transpose(2, 0, 1)
        elif name in ("L0_attn_b1", "L3_ffn_b1"):
            a = a.reshape(EXPERTS * FB, 128).T
        elif name == "L0_ffn_b1":
            a = a.reshape(FB, 128).T
        elif name == "L1_ffn_bias1":
            a = a.reshape(-1, 128).T
        arrays[name] = a
    arrays.update(constants())
    arrays = {k: np.ascontiguousarray(v) for k, v in arrays.items()}
    dram = {k: nc.dram_tensor(f"in_{k}", a.shape, mybir.dt.from_np(a.dtype), kind="ExternalInput").ap()
            for k, a in arrays.items()}
    dram["out"] = nc.dram_tensor("out_dram", (TOKENS, D), F32, kind="ExternalOutput").ap()
    build_program(nc, dram)
    r = _run(nc, [{f"in_{k}": a for k, a in arrays.items()}], core_ids=[0])
    return r.results[0]["out_dram"].reshape(B, S, D)
```
